# Optimizing a Trainium2 kernel written in Bass

```python
import numpy as np
import jax
import jax.numpy as jnp

def _softmax(x, axis=-1):
    return jax.nn.softmax(x, axis=axis)

def _gelu(x):
    return jax.nn.gelu(x, approximate=True)

def _silu(x):
    return jax.nn.silu(x)

def _sigmoid(x):
    return jax.nn.sigmoid(x)

def _layernorm(x, axis=-1, eps=1e-05):
    m = jnp.mean(x, axis=axis, keepdims=True)
    v = jnp.var(x, axis=axis, keepdims=True)
    return (x - m) / jnp.sqrt(v + eps)

def _scatter_add(tgt, idx, src, axis=0):
    return tgt.at[idx].add(src)

def _segment_sum(src, seg, n):
    return jax.ops.segment_sum(src, seg, n)
kernel_name = 'mk_gnn_resnorm_d2_gnn_r32_a20d9f'

def setup_inputs(seed: int=0):
    np.random.seed(seed)
    _w = jnp.asarray

    def _rec_inputs():
        import jax
        import jax.numpy as jnp
        _gk = jax.random.key(seed)
        x = -0.0001006 + 1 * jax.random.normal(jax.random.fold_in(_gk, 1), (50000, 96), jnp.float32)
        src = jax.random.randint(jax.random.fold_in(_gk, 2), (50000,), 0, 50000, jnp.int32)
        dst = jnp.minimum((50000 * jax.random.uniform(jax.random.fold_in(_gk, 3), (50000,)) ** 2.0).astype(jnp.int32), 49999)
        _o = jnp.argsort(dst, stable=True)
        src = src[_o]
        dst = dst[_o]
        edge_attr_96 = 5.93493e-05 + 1.00006 * jax.random.normal(jax.random.fold_in(_gk, 11), (50000, 96), jnp.float32)
        edge_weight = jax.random.uniform(jax.random.fold_in(_gk, 13), (50000,), jnp.float32, 0.0, 0.999998)
        return (x, src, dst, edge_attr_96, edge_weight)
    x, src, dst, edge_attr_96, edge_weight = _rec_inputs()

    def _L0_gnn_setup():
        import jax, jax.numpy as jnp
        import numpy as np
        N_NODES = 50000
        N_EDGES = 25000
        NIN = 96
        NOUT = 96
        key = jax.random.key(seed)
        ks = jax.random.split(key, 10)
        s = 1.0 / np.sqrt(NIN)
        so = 1.0 / np.sqrt(NOUT)
        return {'x': jax.random.normal(ks[0], (N_NODES, NIN), dtype=jnp.float32), 'edge_index': jax.random.randint(ks[1], (2, N_EDGES), 0, N_NODES, dtype=jnp.int64), 'edge_attr': jax.random.normal(ks[2], (N_EDGES, NIN), dtype=jnp.float32), 'W_edge': jax.random.uniform(ks[3], (NIN, NIN), jnp.float32, -s, s), 'b_edge': jax.random.uniform(ks[4], (NIN,), jnp.float32, -s, s), 'eps': jnp.zeros((), dtype=jnp.float32), 'W1': jax.random.uniform(ks[5], (NOUT, NIN), jnp.float32, -s, s), 'b1': jax.random.uniform(ks[6], (NOUT,), jnp.float32, -s, s), 'W2': jax.random.uniform(ks[7], (NOUT, NOUT), jnp.float32, -so, so), 'b2': jax.random.uniform(ks[8], (NOUT,), jnp.float32, -so, so)}
    _L0_gnn_all = _L0_gnn_setup()
    _L0_gnn_in = {k: v for k, v in _L0_gnn_all.items() if k in ('W_edge', 'b_edge', 'eps', 'W1', 'b1', 'W2', 'b2')}
    del _L0_gnn_all

    def _L1_gnn_setup():
        import jax, jax.numpy as jnp
        import numpy as np
        N_NODES = 50000
        N_EDGES = 25000
        D_FEAT = 96
        key = jax.random.key(seed)
        k1, k2, k3 = jax.random.split(key, 3)
        X = jax.random.normal(k1, (N_NODES, D_FEAT), dtype=jnp.float32)
        edge_index = jax.random.randint(k2, (2, N_EDGES), 0, N_NODES, dtype=jnp.int64)
        edge_weight = jax.random.uniform(k3, (N_EDGES,), dtype=jnp.float32)
        return {'X': X, 'edge_index': edge_index, 'edge_weight': edge_weight}
    _L1_gnn_all = _L1_gnn_setup()
    _L1_gnn_in = {k: v for k, v in _L1_gnn_all.items() if k in ()}
    del _L1_gnn_all
    return {'x': x, 'src': src, 'dst': dst, 'edge_attr_96': edge_attr_96, 'edge_weight': edge_weight, 'L0_gnn_W_edge': _L0_gnn_in['W_edge'], 'L0_gnn_b_edge': _L0_gnn_in['b_edge'], 'L0_gnn_eps': _L0_gnn_in['eps'], 'L0_gnn_W1': _L0_gnn_in['W1'], 'L0_gnn_b1': _L0_gnn_in['b1'], 'L0_gnn_W2': _L0_gnn_in['W2'], 'L0_gnn_b2': _L0_gnn_in['b2']}

def reference(x, src, dst, edge_attr_96, edge_weight, L0_gnn_W_edge, L0_gnn_b_edge, L0_gnn_eps, L0_gnn_W1, L0_gnn_b1, L0_gnn_W2, L0_gnn_b2):
    import jax
    import jax.numpy as jnp

    def _L0_gnn_ref(x, edge_index, edge_attr, W_edge, b_edge, eps, W1, b1, W2, b2):
        import jax, jax.numpy as jnp
        import numpy as np
        N_NODES = 50000
        N_EDGES = 25000
        NIN = 96
        NOUT = 96
        ea = edge_attr @ W_edge.T + b_edge
        src, dst = (edge_index[0], edge_index[1])
        msg = jax.nn.relu(x[src] + ea)
        aggr = jax.ops.segment_sum(msg, dst, num_segments=N_NODES)
        h = (1.0 + eps) * x + aggr
        h = jax.nn.relu(h @ W1.T + b1)
        return h @ W2.T + b2

    def _L1_gnn_ref(X, edge_index, edge_weight):
        import jax, jax.numpy as jnp
        import numpy as np
        N_NODES = 50000
        N_EDGES = 25000
        D_FEAT = 96
        dst, src = (edge_index[0], edge_index[1])
        messages = edge_weight[:, None] * X[src]
        out = jax.ops.segment_sum(messages, dst, num_segments=X.shape[0])
        return out
    edge_index = jnp.stack([src, dst])
    x = _layernorm(x + _L0_gnn_ref(x, edge_index, edge_attr_96, L0_gnn_W_edge, L0_gnn_b_edge, L0_gnn_eps, L0_gnn_W1, L0_gnn_b1, L0_gnn_W2, L0_gnn_b2), axis=-1)
    x = _layernorm(x + _L1_gnn_ref(x, edge_index, edge_weight), axis=-1)
    return x

_drawn_inputs = setup_inputs


def setup_inputs(seed=0):
    import zlib

    import numpy as np

    out = dict(_drawn_inputs(seed))
    spreads = {}
    factors = {'L0_gnn_b_edge': 3.245}
    for name, (base, spread) in spreads.items():
        noise = np.random.default_rng([zlib.crc32(name.encode()), seed]).standard_normal(out[name].shape)
        drawn = base * np.exp(spread * noise) if base else spread * noise
        out[name] = jnp.asarray(drawn.astype(out[name].dtype))
    for name, factor in factors.items():
        out[name] = (out[name] * factor).astype(out[name].dtype)
    return out
```

```python
import concourse.bass as bass
from concourse import mybir
from contextlib import ExitStack


def gnn_kernel(nc, x, src, dst, edge_attr, edge_weight, w_edge_t, b_edge, eps, w1_t, b1, w2_t, b2, out):
    fp32 = mybir.dt.float32
    i32 = mybir.dt.int32
    ALU = mybir.AluOpType
    ACT = mybir.ActivationFunctionType
    AX = mybir.AxisListType

    N, D = x.shape
    E = src.shape[0]
    assert N == E
    P = 128
    G = 5
    BLK = G * P
    NB = N // BLK
    TAIL = N - NB * BLK
    PAIRS = NB // 2
    assert NB % 2 == 0 and 0 < TAIL <= P
    SPARE = BLK
    LN_EPS = 1e-5
    BANK = 512

    def full(a, width):
        return a[0:NB * BLK, :].rearrange("(b p g) d -> b p (g d)", p=P, g=G)

    def last(a):
        return a[NB * BLK:N, :]

    col = lambda a: a.rearrange("(n o) -> n o", o=1)
    src_c, dst_c, w_c = col(src), col(dst), col(edge_weight)

    agg0 = nc.dram_tensor("agg0", [N + SPARE, D], fp32, kind="Internal").ap()
    h_all = nc.dram_tensor("h_all", [N, D], fp32, kind="Internal").ap()
    agg1 = nc.dram_tensor("agg1", [N + SPARE, D], fp32, kind="Internal").ap()

    ctx = ExitStack()
    with ctx:
        def sb(name, shape, dt=fp32):
            return ctx.enter_context(nc.sbuf_tensor(name, shape, dt))

        def pb(name, shape):
            return ctx.enter_context(nc.psum_tensor(name, shape, fp32))

        def sem(name):
            return ctx.enter_context(nc.semaphore(name))

        ident = sb("ident", [P, P])
        after = sb("after", [P, BLK])
        spare_f = sb("spare_f", [P, G])
        spare_i = sb("spare_i", [P, G], i32)
        we = sb("we", [D + 1, D])
        w1 = sb("w1", [D, D])
        w2 = sb("w2", [D + 1, D])
        b1c = sb("b1c", [D, 1])
        eps1 = sb("eps1", [P, 1])
        lneps = sb("lneps", [P, 1])
        zeros = sb("zeros", [P, 4800])

        key_col = sb("key_col", [P, 2, G], i32)
        key_row = sb("key_row", [P, 2, BLK], i32)
        get_col = sb("get_col", [P, 2, G], i32)
        wgt = sb("wgt", [P, 2, G])
        attr = sb("attr", [P, 2, G * D])
        attr_t = [sb(f"attr_t{s}", [D + 1, BLK]) for s in range(2)]
        got = sb("got", [P, 2, G * D])
        pre = sb("pre", [P, 2, G * D])
        msg = sb("msg", [P, 2, G * D])
        same = sb("same", [P, 2, G * BLK])
        count = sb("count", [P, 2, G])
        is_last = sb("is_last", [P, 2, G])
        off_spare = sb("off_spare", [P, 2, G])
        off_last = sb("off_last", [P, 2, G])
        put_col = sb("put_col", [P, 2, G], i32)
        sums = sb("sums", [P, 2, G * D])

        xin = sb("xin", [P, 2, G * D])
        ain = sb("ain", [P, 2, G * D])
        hin = sb("hin", [P, 2, G * D])
        h_t = sb("h_t", [D, BLK])
        hid_t = sb("hid_t", [D + 1, BLK])
        y = sb("y", [P, G * D])
        sq = sb("sq", [P, G * D])
        tot = sb("tot", [P, G])
        mean = sb("mean", [P, G])
        var = sb("var", [P, G])
        std = sb("std", [P, G])
        rstd = sb("rstd", [P, G])
        res = sb("res", [P, 2, G * D])

        wide = [pb(f"wide{s}", [P, 2 * BANK]) for s in range(2)]
        mid = [pb(f"mid{s}", [P, BANK]) for s in range(2)]
        tot_ps = [pb(f"tot_ps{s}", [P, BANK]) for s in range(2)]

        s_pool_go = sem("s_pool_go")
        s_sp_go = sem("s_sp_go")
        s_wts = sem("s_wts")
        s_const = sem("s_const")
        s_iota = sem("s_iota")
        s_spare = sem("s_spare")
        s_eps = sem("s_eps")
        s_zero = sem("s_zero")
        s_cleared = sem("s_cleared")
        s_ones = sem("s_ones")

        class Edge:
            def __init__(self, tag):
                self.key_in = [sem(f"{tag}_key_in{s}") for s in range(2)]
                self.get_in = [sem(f"{tag}_get_in{s}") for s in range(2)]
                self.load_in = [sem(f"{tag}_load_in{s}") for s in range(2)]
                self.got_in = [sem(f"{tag}_got_in{s}") for s in range(2)]
                self.put_done = [sem(f"{tag}_put_done{s}") for s in range(2)]
                self.matched = sem(f"{tag}_matched")
                self.dve = sem(f"{tag}_dve")
                self.put_ready = sem(f"{tag}_put_ready")
                self.attr_tp = sem(f"{tag}_attr_tp")
                self.attr_ts = sem(f"{tag}_attr_ts")
                self.ea_mm = sem(f"{tag}_ea_mm")
                self.added = sem(f"{tag}_added")
                self.msg_ready = sem(f"{tag}_msg_ready")
                self.sum_mm = sem(f"{tag}_sum_mm")
                self.sums_ready = sem(f"{tag}_sums_ready")

        class Node:
            def __init__(self, tag):
                self.x_in = [sem(f"{tag}_x_in{s}") for s in range(2)]
                self.stored = [sem(f"{tag}_stored{s}") for s in range(2)]
                self.h = sem(f"{tag}_h")
                self.tp = sem(f"{tag}_tp")
                self.ts = sem(f"{tag}_ts")
                self.hid_mm = sem(f"{tag}_hid_mm")
                self.hid = sem(f"{tag}_hid")
                self.out_mm = sem(f"{tag}_out_mm")
                self.y = sem(f"{tag}_y")
                self.tot = sem(f"{tag}_tot")
                self.mean = sem(f"{tag}_mean")
                self.cent = sem(f"{tag}_cent")
                self.sq = sem(f"{tag}_sq")
                self.var = sem(f"{tag}_var")
                self.std = sem(f"{tag}_std")
                self.rstd = sem(f"{tag}_rstd")
                self.res = sem(f"{tag}_res")

        e0, e1 = Edge("e0"), Edge("e1")
        n0, n1 = Node("n0"), Node("n1")

        def had(i, s, back):
            return not isinstance(i, int) or 2 * i + s >= back

        def skewed(eng, lead, follow):
            lead(0, 0, G, P)

            def pair(i):
                lead(i, 1, G, P)
                follow(i, 0, G, P)
                lead(i + 1, 0, G, P)
                follow(i, 1, G, P)

            pair(0)
            with eng.Fori(1, PAIRS - 1) as i:
                pair(i)
            lead(PAIRS - 1, 1, G, P)
            follow(PAIRS - 1, 0, G, P)
            lead(PAIRS, 0, 1, TAIL)
            follow(PAIRS - 1, 1, G, P)
            follow(PAIRS, 0, 1, TAIL)

        def straight(eng, step):
            step(0, 0, G, P)
            step(0, 1, G, P)
            with eng.Fori(1, PAIRS) as i:
                step(i, 0, G, P)
                step(i, 1, G, P)
            step(PAIRS, 0, 1, TAIL)

        def dram(a, i, s, tiles):
            return full(a, None)[2 * i + s, :, :] if tiles == G else last(a)

        def row_of(a, i, s, tiles):
            flat = a.rearrange("(o n) -> o n", o=1)
            if tiles == G:
                r = a[0:NB * BLK].rearrange("(b o n) -> b o n", o=1, n=BLK)[2 * i + s, :, :]
                return r.to_broadcast([P, BLK])
            return flat[:, NB * BLK:N].to_broadcast([TAIL, TAIL])

        def slot_total(i, n, tiles, m=None):
            return 16 * n * (i + 1) if tiles == G else 16 * n * i + 16 * (n if m is None else m)

        CW = 4800
        chunks = []
        at, total = 0, (N + SPARE) * D
        flat0 = agg0.rearrange("n d -> (n d)")
        while at < total:
            w = min(CW, (total - at) // P)
            chunks.append((at, w))
            at += P * w
        assert at == total
        CLEARS = len(chunks) + 1

        block = ctx.enter_context(nc.Block())

        @block.sync
        def _(sp):
            sp.dma_start(we[0:D, :], w_edge_t).then_inc(s_wts, 16)
            sp.dma_start(we[D:D + 1, :], b_edge).then_inc(s_wts, 16)
            sp.dma_start(w1[:, :], w1_t).then_inc(s_wts, 16)
            sp.dma_start(w2[0:D, :], w2_t).then_inc(s_wts, 16)
            sp.dma_start(w2[D:D + 1, :], b2).then_inc(s_wts, 16)
            sp.dma_start(b1c[:, :], b1).then_inc(s_wts, 16)
            sp.dma_start(eps1[:, :], eps.to_broadcast([P, 1])).then_inc(s_wts, 16)

            def load_edges(e, key_1d, get_1d, key, get, i, s, tiles, rows):
                w = tiles
                if had(i, s, 2):
                    used = 16 * G * i
                    done = 2 * i + s - 1
                    sp.wait_ge(e.put_ready, done)
                    if e is e0:
                        sp.wait_ge(e.attr_tp, done)
                    else:
                        sp.wait_ge(e.msg_ready, done)
                    sp.sem_inc(s_sp_go, 1)
                    sp.wait_ge(e.got_in[s], used)
                sp.dma_start(get_col[0:rows, s, 0:w], dram(get, i, s, tiles)).then_inc(e.get_in[s], 16)
                sp.dma_start(key_col[0:rows, s, 0:w], dram(key, i, s, tiles)).then_inc(e.key_in[s], 16)
                sp.dma_start(key_row[0:rows, s, 0:tiles * rows],
                             row_of(key_1d, i, s, tiles)).then_inc(e.key_in[s], 16)
                if e is e0:
                    sp.dma_start(attr[0:rows, s, 0:w * D],
                                 dram(edge_attr, i, s, tiles)).then_inc(e.load_in[s], 16)
                else:
                    sp.dma_start(wgt[0:rows, s, 0:w], dram(w_c, i, s, tiles)).then_inc(e.load_in[s], 16)

            straight(sp, lambda *b: load_edges(e0, dst, src, dst_c, src_c, *b))

            sp.wait_ge(e0.put_done[1], 16 * G * PAIRS)
            sp.wait_ge(e0.put_done[0], 16 * G * PAIRS + 16)

            def load_nodes(i, s, tiles, rows):
                if had(i, s, 2):
                    sp.wait_ge(n0.y, 2 * i + s - 1)
                sp.dma_start(xin[0:rows, s, 0:tiles * D], dram(x, i, s, tiles)).then_inc(n0.x_in[s], 16)
                sp.dma_start(ain[0:rows, s, 0:tiles * D], dram(agg0[0:N, :], i, s, tiles)).then_inc(n0.x_in[s], 16)

            straight(sp, load_nodes)
            straight(sp, lambda *b: load_edges(e1, src, dst, src_c, dst_c, *b))

            sp.wait_ge(e1.put_done[1], 16 * G * PAIRS)
            sp.wait_ge(e1.put_done[0], 16 * G * PAIRS + 16)

            def load_final(i, s, tiles, rows):
                if had(i, s, 2):
                    sp.wait_ge(n1.cent, 2 * i + s - 1)
                sp.dma_start(ain[0:rows, s, 0:tiles * D], dram(agg1[0:N, :], i, s, tiles)).then_inc(n1.x_in[s], 16)

            straight(sp, load_final)

        @block.gpsimd
        def _(pool):
            nc.gpsimd.memset(ident[:, :], 1.0).then_inc(s_const, 1)
            nc.gpsimd.memset(after[:, :], 1.0).then_inc(s_const, 1)
            pool.wait_ge(s_const, 2)
            nc.gpsimd.affine_select(out=ident[:, :], in_=ident[:, :], compare_op=ALU.is_equal, fill=0.0,
                                    base=0, pattern=[[-1, P]], channel_multiplier=1).then_inc(s_const, 1)
            nc.gpsimd.affine_select(out=after[:, :], in_=after[:, :], compare_op=ALU.is_ge, fill=0.0,
                                    base=0, pattern=[[1, BLK]], channel_multiplier=-1).then_inc(s_const, 1)
            nc.gpsimd.iota(spare_i[:, :], pattern=[[P, G]], base=N, channel_multiplier=1).then_inc(s_iota, 1)

            def gather(e, table, i, s, tiles, rows):
                if had(i, s, 2):
                    used = 2 * i + s - 1
                loaded = 16 * (i + 1)
                pool.wait_ge(e.get_in[s], loaded)
                if had(i, s, 2):
                    pool.wait_ge(e.added if e is e0 else e.msg_ready, used)
                pool.sem_inc(s_pool_go, 1)
                for g in range(tiles):
                    nc.gpsimd.indirect_dma_start(
                        got[0:rows, s, g * D:(g + 1) * D], None, table,
                        bass.IndirectOffsetOnAxis(ap=get_col[0:rows, s, g:g + 1], axis=0),
                    ).then_inc(e.got_in[s], 16)

            def scatter(e, table, i, s, tiles, rows):
                ready = 2 * i + s + 1
                landed = 16 * G * (i + s)
                pool.wait_ge(s_cleared, 16 * CLEARS)
                if had(i, s, 1):
                    pool.wait_ge(e.put_done[1 - s], landed)
                pool.wait_ge(e.put_ready, ready)
                pool.wait_ge(e.sums_ready, ready)
                pool.sem_inc(s_pool_go, 1)
                for g in range(tiles):
                    nc.gpsimd.indirect_dma_start(
                        table, bass.IndirectOffsetOnAxis(ap=put_col[0:rows, s, g:g + 1], axis=0),
                        sums[0:rows, s, g * D:(g + 1) * D], None, compute_op=ALU.add,
                    ).then_inc(e.put_done[s], 16)

            skewed(pool, lambda *b: gather(e0, x, *b), lambda *b: scatter(e0, agg0, *b))
            pool.wait_ge(n0.stored[1], 32 * PAIRS)
            pool.wait_ge(n0.stored[0], 32 * PAIRS + 32)
            skewed(pool, lambda *b: gather(e1, h_all, *b), lambda *b: scatter(e1, agg1, *b))

        @block.scalar
        def _(act):
            act.wait_ge(s_zero, 1)
            for at, w in chunks:
                act.dma_start(flat0[at:at + P * w].rearrange("(p w) -> p w", p=P), zeros[:, 0:w]).then_inc(s_cleared, 16)
            act.dma_start(agg1[N:N + SPARE, :].rearrange("(p g) d -> p (g d)", p=P),
                          zeros[:, 0:SPARE // P * D]).then_inc(s_cleared, 16)

            def attr_to_sbuf(i, s, tiles, rows):
                act.wait_ge(e0.attr_tp, 2 * i + s + 1)
                if had(i, s, 2):
                    act.wait_ge(e0.ea_mm, 2 * i + s - 1)
                nc.scalar.copy(attr_t[s][0:D, 0:(tiles - 1) * P + rows],
                               wide[s][0:D, 0:(tiles - 1) * P + rows]).then_inc(e0.attr_ts, 1)

            def sums_to_sbuf(e, i, s, tiles, rows):
                act.wait_ge(e.sum_mm, 2 * i + s + 1)
                if had(i, s, 2):
                    act.wait_ge(e.put_done[s], 16 * G * i)
                nc.scalar.copy(sums[0:rows, s, 0:tiles * D], tot_ps[s][0:rows, 0:tiles * D]).then_inc(e.sums_ready, 1)

            def messages(i, s, tiles, rows):
                act.wait_ge(e0.added, 2 * i + s + 1)
                if had(i, s, 2):
                    act.wait_ge(e0.sum_mm, 2 * i + s - 1)
                nc.scalar.activation(msg[0:rows, s, 0:tiles * D], pre[0:rows, s, 0:tiles * D],
                                     ACT.Relu).then_inc(e0.msg_ready, 1)
                sums_to_sbuf(e0, i, s, tiles, rows)

            skewed(act, attr_to_sbuf, messages)

            def to_sbuf(i, s, tiles, rows):
                m = (tiles - 1) * P + rows
                act.wait_ge(n0.tp, 2 * i + s + 1)
                if had(i, s, 1):
                    act.wait_ge(n0.hid_mm, 2 * i + s)
                nc.scalar.copy(h_t[:, 0:m], wide[0][0:D, 0:m]).then_inc(n0.ts, 1)
                act.wait_ge(n0.hid_mm, 2 * i + s + 1)
                if had(i, s, 1):
                    act.wait_ge(n0.out_mm, 2 * i + s)
                nc.scalar.activation(hid_t[0:D, 0:m], wide[1][0:D, 0:m], ACT.Relu,
                                     bias=b1c[:, 0:1]).then_inc(n0.hid, 1)

            def norm(n, i, s, tiles, rows):
                act.wait_ge(n.cent, 2 * i + s + 1)
                if had(i, s, 1):
                    act.wait_ge(n.var, 2 * i + s)
                nc.scalar.activation(sq[0:rows, 0:tiles * D], y[0:rows, 0:tiles * D], ACT.Square).then_inc(n.sq, 1)
                act.wait_ge(n.var, 2 * i + s + 1)
                if had(i, s, 1):
                    act.wait_ge(n.rstd, 2 * i + s)
                nc.scalar.activation(std[0:rows, 0:tiles], var[0:rows, 0:tiles], ACT.Sqrt,
                                     bias=lneps[0:rows, 0:1], scale=1.0 / D).then_inc(n.std, 1)

            def store(n, tables, i, s, tiles, rows):
                act.wait_ge(n.res, 2 * i + s + 1)
                for t in tables:
                    act.dma_start(dram(t, i, s, tiles), res[0:rows, s, 0:tiles * D]).then_inc(n.stored[s], 16)

            def norm_and_store0(*b):
                norm(n0, *b)
                store(n0, (h_all, agg1[0:N, :]), *b)

            act.wait_ge(s_eps, 1)
            skewed(act, to_sbuf, norm_and_store0)
            straight(act, lambda *b: sums_to_sbuf(e1, *b))

            def norm_and_store1(*b):
                norm(n1, *b)
                store(n1, (out,), *b)

            straight(act, norm_and_store1)
            act.wait_ge(n1.stored[1], 16 * PAIRS)
            act.wait_ge(n1.stored[0], 16 * PAIRS + 16)

        @block.vector
        def _(dve):
            nc.vector.memset(zeros[:, :], 0.0).then_inc(s_zero, 1)
            nc.vector.memset(attr_t[0][D:D + 1, :], 1.0).then_inc(s_ones, 1)
            nc.vector.memset(attr_t[1][D:D + 1, :], 1.0).then_inc(s_ones, 1)
            nc.vector.memset(hid_t[D:D + 1, :], 1.0).then_inc(s_ones, 1)
            nc.vector.memset(lneps[:, :], LN_EPS).then_inc(s_eps, 1)
            dve.wait_ge(s_iota, 1)
            nc.vector.tensor_copy(spare_f[:, :], spare_i[:, :]).then_inc(s_spare, 1)
            dve.wait_ge(s_wts, 16 * 7)
            nc.vector.tensor_scalar(eps1[:, :], eps1[:, :], 1.0, None, ALU.add).then_inc(s_spare, 1)
            dve.wait_ge(s_spare, 2)
            dve.wait_ge(s_const, 4)

            def match(e, i, s, tiles, rows):
                dve.wait_ge(e.key_in[s], 32 * (i + 1))
                if had(i, s, 2):
                    dve.wait_ge(e.sum_mm, 2 * i + s - 1)
                    dve.wait_ge(e.put_done[s], 16 * G * i)
                by_tile = key_row[0:rows, s, 0:tiles * rows].rearrange("k (p g) -> k g p", g=tiles)
                for g in range(tiles):
                    m = tiles - g
                    ins = nc.vector.scalar_tensor_tensor(
                        out=same[0:rows, s, g * BLK + g * P:g * BLK + g * P + (m - 1) * P + rows]
                            .rearrange("k (g p) -> k g p", g=m),
                        in0=by_tile[:, g:, :], scalar=key_col[0:rows, s, g:g + 1],
                        in1=after[0:rows, 0:(m - 1) * P + rows].rearrange("k (g p) -> k g p", g=m),
                        op0=ALU.is_equal, op1=ALU.mult, accum_out=count[0:rows, s, g:g + 1])
                ins.then_inc(e.matched, 1)
                dve.wait_ge(e.matched, 2 * i + s + 1)
                nc.vector.tensor_scalar(is_last[0:rows, s, 0:tiles], count[0:rows, s, 0:tiles], 1.0, None,
                                        ALU.is_equal)
                nc.vector.tensor_tensor(off_spare[0:rows, s, 0:tiles], key_col[0:rows, s, 0:tiles],
                                        spare_f[0:rows, 0:tiles], ALU.subtract).then_inc(e.dve, 1)
                dve.wait_ge(e.dve, 4 * i + 2 * s + 1)
                nc.vector.tensor_tensor(off_last[0:rows, s, 0:tiles], off_spare[0:rows, s, 0:tiles],
                                        is_last[0:rows, s, 0:tiles], ALU.mult).then_inc(e.dve, 1)
                dve.wait_ge(e.dve, 4 * i + 2 * s + 2)
                nc.vector.tensor_tensor(put_col[0:rows, s, 0:tiles], off_last[0:rows, s, 0:tiles],
                                        spare_f[0:rows, 0:tiles], ALU.add).then_inc(e.put_ready, 1)

            def got_total(i, s, tiles):
                return 16 * G * (i + 1) if tiles == G else 16 * G * i + 16

            def add(i, s, tiles, rows):
                dve.wait_ge(e0.ea_mm, 2 * i + s + 1)
                dve.wait_ge(e0.got_in[s], got_total(i, s, tiles))
                if had(i, s, 2):
                    dve.wait_ge(e0.msg_ready, 2 * i + s - 1)
                nc.vector.tensor_tensor(pre[0:rows, s, 0:tiles * D], mid[s][0:rows, 0:tiles * D],
                                        got[0:rows, s, 0:tiles * D], ALU.add).then_inc(e0.added, 1)

            skewed(dve, lambda *b: match(e0, *b), add)

            def form_h(i, s, tiles, rows):
                dve.wait_ge(n0.x_in[s], 32 * (i + 1))
                if had(i, s, 2):
                    dve.wait_ge(n0.tp, 2 * i + s - 1)
                nc.vector.scalar_tensor_tensor(
                    out=hin[0:rows, s, 0:tiles * D], in0=xin[0:rows, s, 0:tiles * D], scalar=eps1[0:rows, 0:1],
                    in1=ain[0:rows, s, 0:tiles * D], op0=ALU.mult, op1=ALU.add).then_inc(n0.h, 1)

            def norm(n, values, i, s, tiles, rows):
                cut = lambda a: a[0:rows, 0:tiles * D].rearrange("p (g d) -> p g d", g=tiles)
                wide_of = lambda a: a[0:rows, 0:tiles].unsqueeze(2).to_broadcast([rows, tiles, D])
                nc.vector.tensor_reduce(out=tot[0:rows, 0:tiles], in_=cut(values), axis=AX.X, op=ALU.add).then_inc(n.tot, 1)
                dve.wait_ge(n.tot, 2 * i + s + 1)
                nc.vector.tensor_scalar(mean[0:rows, 0:tiles], tot[0:rows, 0:tiles], 1.0 / D, None,
                                        ALU.mult).then_inc(n.mean, 1)
                dve.wait_ge(n.mean, 2 * i + s + 1)
                nc.vector.tensor_tensor(cut(y), cut(values), wide_of(mean), ALU.subtract).then_inc(n.cent, 1)
                dve.wait_ge(n.sq, 2 * i + s + 1)
                nc.vector.tensor_reduce(out=var[0:rows, 0:tiles], in_=cut(sq), axis=AX.X, op=ALU.add).then_inc(n.var, 1)
                dve.wait_ge(n.std, 2 * i + s + 1)
                nc.vector.reciprocal(rstd[0:rows, 0:tiles], std[0:rows, 0:tiles]).then_inc(n.rstd, 1)
                dve.wait_ge(n.rstd, 2 * i + s + 1)
                if had(i, s, 2):
                    dve.wait_ge(n.stored[s], (32 if n is n0 else 16) * i)
                nc.vector.tensor_tensor(cut(res[:, s, :]), cut(y), wide_of(rstd), ALU.mult).then_inc(n.res, 1)
                dve.wait_ge(n.res, 2 * i + s + 1)

            def finish0(i, s, tiles, rows):
                dve.wait_ge(n0.out_mm, 2 * i + s + 1)
                nc.vector.tensor_tensor(y[0:rows, 0:tiles * D], mid[s][0:rows, 0:tiles * D],
                                        xin[0:rows, s, 0:tiles * D], ALU.add).then_inc(n0.y, 1)
                dve.wait_ge(n0.y, 2 * i + s + 1)
                norm(n0, y, i, s, tiles, rows)

            skewed(dve, form_h, finish0)

            def weigh(i, s, tiles, rows):
                dve.wait_ge(e1.load_in[s], 16 * (i + 1))
                dve.wait_ge(e1.got_in[s], got_total(i, s, tiles))
                if had(i, s, 2):
                    dve.wait_ge(e1.sum_mm, 2 * i + s - 1)
                nc.vector.tensor_tensor(
                    msg[0:rows, s, 0:tiles * D].rearrange("p (g d) -> p g d", g=tiles),
                    got[0:rows, s, 0:tiles * D].rearrange("p (g d) -> p g d", g=tiles),
                    wgt[0:rows, s, 0:tiles].unsqueeze(2).to_broadcast([rows, tiles, D]), ALU.mult).then_inc(e1.msg_ready, 1)

            skewed(dve, lambda *b: match(e1, *b), weigh)

            def finish1(i, s, tiles, rows):
                dve.wait_ge(n1.x_in[s], 16 * (i + 1))
                norm(n1, ain[:, s, :], i, s, tiles, rows)

            straight(dve, finish1)

        @block.tensor
        def _(pe):
            pe.wait_ge(s_const, 4)
            pe.wait_ge(s_wts, 16 * 7)
            pe.wait_ge(s_ones, 3)

            def edge_linear(i, s, tiles, rows):
                pe.wait_ge(e0.load_in[s], 16 * (i + 1))
                if had(i, s, 2):
                    pe.wait_ge(e0.attr_ts, 2 * i + s - 1)
                for g in range(tiles):
                    ins = nc.tensor.transpose(wide[s][0:D, g * P:g * P + rows], attr[0:rows, s, g * D:(g + 1) * D],
                                              ident[0:rows, 0:rows])
                ins.then_inc(e0.attr_tp, 1)
                pe.wait_ge(e0.attr_ts, 2 * i + s + 1)
                if had(i, s, 2):
                    pe.wait_ge(e0.added, 2 * i + s - 1)
                for g in range(tiles):
                    ins = nc.tensor.matmul(mid[s][0:rows, g * D:(g + 1) * D], attr_t[s][:, g * P:g * P + rows],
                                           we[:, :], start=True, stop=True)
                ins.then_inc(e0.ea_mm, 1)

            def block_sums(e, i, s, tiles, rows):
                pe.wait_ge(e.matched, 2 * i + s + 1)
                pe.wait_ge(e.msg_ready, 2 * i + s + 1)
                if had(i, s, 2):
                    pe.wait_ge(e.sums_ready, 2 * i + s - 1)
                for g in range(tiles):
                    for k in range(g + 1):
                        ins = nc.tensor.matmul(tot_ps[s][0:rows, g * D:(g + 1) * D],
                                               same[0:rows, s, k * BLK + g * P:k * BLK + g * P + rows],
                                               msg[0:rows, s, k * D:(k + 1) * D], start=(k == 0), stop=(k == g))
                ins.then_inc(e.sum_mm, 1)

            skewed(pe, edge_linear, lambda *b: block_sums(e0, *b))

            def hidden(i, s, tiles, rows):
                m = (tiles - 1) * P + rows
                pe.wait_ge(n0.h, 2 * i + s + 1)
                if had(i, s, 1):
                    pe.wait_ge(n0.ts, 2 * i + s)
                for g in range(tiles):
                    ins = nc.tensor.transpose(wide[0][0:D, g * P:g * P + rows], hin[0:rows, s, g * D:(g + 1) * D],
                                              ident[0:rows, 0:rows])
                ins.then_inc(n0.tp, 1)
                pe.wait_ge(n0.ts, 2 * i + s + 1)
                if had(i, s, 1):
                    pe.wait_ge(n0.hid, 2 * i + s)
                for at in range(0, m, BANK):
                    to = min(m, at + BANK)
                    ins = nc.tensor.matmul(wide[1][0:D, at:to], w1[:, :], h_t[:, at:to], start=True, stop=True)
                ins.then_inc(n0.hid_mm, 1)

            def project(i, s, tiles, rows):
                pe.wait_ge(n0.hid, 2 * i + s + 1)
                if had(i, s, 2):
                    pe.wait_ge(n0.y, 2 * i + s - 1)
                for g in range(tiles):
                    ins = nc.tensor.matmul(mid[s][0:rows, g * D:(g + 1) * D], hid_t[:, g * P:g * P + rows],
                                           w2[:, :], start=True, stop=True)
                ins.then_inc(n0.out_mm, 1)

            straight(pe, lambda *b: (hidden(*b), project(*b)))
            straight(pe, lambda *b: block_sums(e1, *b))


def kernel(x, src, dst, edge_attr_96, edge_weight, L0_gnn_W_edge, L0_gnn_b_edge, L0_gnn_eps, L0_gnn_W1, L0_gnn_b1,
           L0_gnn_W2, L0_gnn_b2):
    import numpy as np
    import concourse.bacc as bacc
    from concourse import mybir as mb
    from concourse.bass_utils import run_bass_kernel_spmd

    laid_out = {
        "x": x, "src": src, "dst": dst, "edge_attr": edge_attr_96, "edge_weight": edge_weight,
        "w_edge_t": np.asarray(L0_gnn_W_edge).T, "b_edge": np.asarray(L0_gnn_b_edge).reshape(1, -1),
        "eps": np.asarray(L0_gnn_eps).reshape(1, 1), "w1_t": np.asarray(L0_gnn_W1).T,
        "b1": np.asarray(L0_gnn_b1).reshape(-1, 1), "w2_t": np.asarray(L0_gnn_W2).T,
        "b2": np.asarray(L0_gnn_b2).reshape(1, -1),
    }
    nc = bacc.Bacc("TRN2", target_bir_lowering=False, num_devices=1)
    arrays, args = {}, []
    for name, a in laid_out.items():
        a = np.ascontiguousarray(a)
        arrays[f"in_{name}"] = a
        args.append(nc.dram_tensor(f"in_{name}", a.shape, mb.dt.from_np(a.dtype), kind="ExternalInput").ap())
    out = nc.dram_tensor("out_h", x.shape, mb.dt.float32, kind="ExternalOutput").ap()
    gnn_kernel(nc, *args, out)
    r = run_bass_kernel_spmd(nc, [arrays], core_ids=[0])
    return r.results[0]["out_h"]
```

```python
import concourse.bass as bass
from concourse import mybir
from contextlib import ExitStack


def gnn_kernel(nc, x, src, dst, edge_attr, edge_weight, w_edge_t, b_edge, eps, w1_t, b1, w2_t, b2, out):
    fp32 = mybir.dt.float32
    i32 = mybir.dt.int32
    ALU = mybir.AluOpType
    ACT = mybir.ActivationFunctionType
    ENG = mybir.EngineType

    N, D = x.shape
    assert N == src.shape[0]
    P = 128
    G = 5
    BLK = G * P
    NB = N // BLK
    TAIL = N - NB * BLK
    NT = NB * G + 1
    PAIRS = NB // 2
    assert NB % 2 == 0 and 0 < TAIL <= P and NB < P
    WIDE, NARROW = 4, 3
    SPARE = BLK
    ENTRY = 8
    SPAN = G
    LN_EPS = 1e-5
    BANK = 512

    def short(i, s):
        return isinstance(i, int) and 2 * i + s == NB

    def by_block(a, i, s):
        if short(i, s):
            return a[NB * BLK:N, :]
        return a[0:NB * BLK, :].rearrange("(b p g) d -> b p (g d)", p=P, g=G)[2 * i + s, :, :]

    def by_tile(a, i, s):
        if short(i, s):
            return a[NB * BLK:N, :].rearrange("(g p) d -> p g d", g=1)
        return a[0:NB * BLK, :].rearrange("(b g p) d -> b p g d", p=P, g=G)[2 * i + s, :, :, :]

    def as_row(a, i, s):
        if short(i, s):
            return a.rearrange("(o n) -> o n", o=1)[:, NB * BLK:N].to_broadcast([TAIL, TAIL])
        r = a[0:NB * BLK].rearrange("(b o n) -> b o n", o=1, n=BLK)[2 * i + s, :, :]
        return r.to_broadcast([P, BLK])

    col = lambda a: a.rearrange("(n o) -> n o", o=1)
    src_c, dst_c, w_c = col(src), col(dst), col(edge_weight)

    table = [nc.dram_tensor(f"table{k}", [N + SPARE, D], fp32, kind="Internal").ap() for k in range(2)]
    h_dram = nc.dram_tensor("h_dram", [N, D], fp32, kind="Internal").ap()
    plan_dram = nc.dram_tensor("plan_dram", [NB + 1, ENTRY], i32, kind="Internal").ap()

    ctx = ExitStack()
    with ctx:
        def sb(name, shape, dt=fp32):
            return ctx.enter_context(nc.sbuf_tensor(name, shape, dt))

        def pb(name, shape):
            return ctx.enter_context(nc.psum_tensor(name, shape, fp32))

        def sem(name):
            return ctx.enter_context(nc.semaphore(name))

        ident = sb("ident", [P, P])
        after = sb("after", [P, BLK], mybir.dt.bfloat16)
        number_i = sb("number_i", [P, G], i32)
        spare_row = sb("spare_row", [P, G])
        window_row = sb("window_row", [P, WIDE])
        count_up = sb("count_up", [P, WIDE * P])
        we = sb("we", [D + 1, D])
        w1 = sb("w1", [D, D])
        w2 = sb("w2", [D + 1, D])
        b1c = sb("b1c", [D, 1])
        eps1 = sb("eps1", [P, 1])
        lneps = sb("lneps", [P, 1])
        zeros = sb("zeros", [P, (TAIL + SPARE) * D // P])
        plan = sb("plan", [P, (NB + 1) * ENTRY], i32)
        span_all = sb("span_all", [1, 1], i32)

        src_col = sb("src_col", [P, (NB + 1) * G])
        dst_col = sb("dst_col", [P, (NB + 1) * G])
        w_col = sb("w_col", [P, (NB + 1) * G])

        nodes = sb("nodes", [P, NT * D])
        WORK = 9600
        work = sb("work", [P, WORK])
        attr_t = [sb(f"attr_t{s}", [D + 1, BLK]) for s in range(2)]
        hid_t = attr_t
        h_t = sb("h_t", [D, BLK])

        key_col = sb("key_col", [P, 2, G], i32)
        get_col = sb("get_col", [P, 2, G], i32)
        wgt = sb("wgt", [P, 2, G])
        local = sb("local", [P, 2, G])
        local_row = sb("local_row", [P, 2, G * WIDE])
        count = sb("count", [P, 2, G])
        is_last = sb("is_last", [P, 2, G])
        off_spare = sb("off_spare", [P, 2, G])
        off_last = sb("off_last", [P, 2, G])
        put_col = sb("put_col", [P, 2, G], i32)
        stats = sb("stats", [P, 2, G * 6])
        mv = sb("mv", [P, 2, G * 2])
        std = sb("std", [P, 2, G])
        rstd = sb("rstd", [P, 2, G])
        shift = sb("shift", [P, 2, G])

        class Area:
            def __init__(self, tensor, at=0):
                self.tensor, self.at = tensor, at

            def take(self, width, dt=fp32):
                a = self.tensor[:, self.at:self.at + 2 * width]
                self.at += 2 * width
                if dt is not fp32:
                    a = a.bitcast(dt)
                return a.rearrange("p (s w) -> p s w", s=2)

        class Buffers:
            pass

        def places(groups):
            found = {}
            for a, z in groups:
                for k in range(a, z):
                    for g in range(k, z):
                        found[k, g] = len(found) * P
            return found

        HOT = WORK - G * WIDE * P
        hot = work[:, HOT:WORK].rearrange("p (g w) -> p g w", g=G)
        F = Buffers()
        F.groups = [(0, 3), (3, G)]
        F.tri = places(F.groups)
        a = Area(work)
        F.attr, F.got, F.pre, F.msg = (a.take(G * D) for _ in range(4))
        assert a.at <= HOT
        a = Area(work)
        F.xin, F.hin, F.y = (a.take(G * D) for _ in range(3))
        a = Area(work)
        F.key_row, F.dst_row, F.same = a.take(BLK, i32), a.take(BLK, i32), a.take(len(F.tri) * P)
        F.msg1, F.sums = a.take(G * D), a.take(G * D)
        assert a.at <= HOT
        a = Area(work)
        F.ain, F.bin, F.ab, F.yf, F.res = (a.take(G * D) for _ in range(5))
        a = Area(nodes)
        M = Buffers()
        M.groups = [(0, G)]
        M.tri = places(M.groups)
        M.attr, M.got, M.pre, M.msg, M.sums = (a.take(G * D) for _ in range(5))
        M.msg1 = M.msg
        M.key_row, M.same = a.take(BLK, i32), a.take(len(M.tri) * P)
        M.xin, M.ain, M.hin, M.y, M.res, M.fin = (a.take(G * D) for _ in range(6))
        assert a.at <= NT * D
        count_i = hot[:, 0, :].bitcast(i32)
        tile_src = work[:, BLK:2 * BLK].bitcast(i32)
        tile_w = work[:, 2 * BLK:3 * BLK]
        tile_f = work[:, 3 * BLK:5 * BLK]
        tile_dst = work[:, 0:BLK].bitcast(i32)
        least = work[:, 3840:3840 + G]
        most = work[:, 3850:3850 + G]
        least_i = work[:, 3860:3860 + G].bitcast(i32)
        most_i = work[:, 3870:3870 + G].bitcast(i32)
        first_i = work[:, 3880:3880 + G].bitcast(i32)
        end_i = work[:, 3890:3890 + G].bitcast(i32)
        spans = work[:, 3900:3900 + G]
        entry = work[:, 3910:3910 + ENTRY].bitcast(i32)

        wide = [pb(f"wide{s}", [P, 2 * BANK]) for s in range(2)]
        mid = [pb(f"mid{s}", [P, BANK]) for s in range(2)]
        tot_ps = [pb(f"tot_ps{s}", [P, BANK]) for s in range(2)]

        s_pool_go = sem("s_pool_go")
        s_sp_go = sem("s_sp_go")
        s_dve_go = sem("s_dve_go")
        s_wts = sem("s_wts")
        s_const = sem("s_const")
        s_iota = sem("s_iota")
        s_number = sem("s_number")
        s_eps = sem("s_eps")
        s_zero = sem("s_zero")
        s_cleared = sem("s_cleared")
        s_nodes0 = sem("s_nodes0")
        s_ones = sem("s_ones")
        s_dst = sem("s_dst")
        s_step = sem("s_step")
        s_rows = sem("s_rows")
        s_float = sem("s_float")
        s_turned = sem("s_turned")
        s_cols = sem("s_cols")
        s_get = sem("s_get")
        s_entry = sem("s_entry")
        s_plan_out = sem("s_plan_out")
        s_plan = sem("s_plan")
        s_span = sem("s_span")

        class Edge:
            def __init__(self, tag):
                two = lambda name: [sem(f"{tag}_{name}{s}") for s in range(2)]
                self.key_in, self.get_in, self.load_in = two("key_in"), two("get_in"), two("load_in")
                self.got_in = two("got_in")
                self.put_done = [two("put_even"), two("put_odd")]
                self.local = sem(f"{tag}_local")
                self.hot = sem(f"{tag}_hot")
                self.win_mm = sem(f"{tag}_win_mm")
                self.win_add = sem(f"{tag}_win_add")
                self.matched = sem(f"{tag}_matched")
                self.dve = sem(f"{tag}_dve")
                self.put_ready = sem(f"{tag}_put_ready")
                self.attr_tp = sem(f"{tag}_attr_tp")
                self.attr_ts = sem(f"{tag}_attr_ts")
                self.ea_mm = sem(f"{tag}_ea_mm")
                self.added = sem(f"{tag}_added")
                self.msg_ready = sem(f"{tag}_msg_ready")
                self.sum_mm = sem(f"{tag}_sum_mm")
                self.sums_ready = sem(f"{tag}_sums_ready")

        class Node:
            def __init__(self, tag):
                two = lambda name: [sem(f"{tag}_{name}{s}") for s in range(2)]
                self.x_in, self.stored = two("x_in"), two("stored")
                self.h = sem(f"{tag}_h")
                self.tp = sem(f"{tag}_tp")
                self.ts = sem(f"{tag}_ts")
                self.hid_mm = sem(f"{tag}_hid_mm")
                self.hid = sem(f"{tag}_hid")
                self.out_mm = sem(f"{tag}_out_mm")
                self.ab = sem(f"{tag}_ab")
                self.y = sem(f"{tag}_y")
                self.stats = sem(f"{tag}_stats")
                self.mv = sem(f"{tag}_mv")
                self.std = sem(f"{tag}_std")
                self.rstd = sem(f"{tag}_rstd")
                self.res = sem(f"{tag}_res")
                self.kept = sem(f"{tag}_kept")
                self.shift = sem(f"{tag}_shift")

        e0, e1 = Edge("e0"), Edge("e1")
        n0, n1 = Node("n0"), Node("n1")

        def had(i, s, back):
            return not isinstance(i, int) or 2 * i + s >= back

        def size(i, s):
            return (1, TAIL) if short(i, s) else (G, P)

        def steps(eng, *stages):
            lead = max(ahead for ahead, _ in stages)
            behind = max(0, -min(ahead for ahead, _ in stages))

            def step(i, s):
                for ahead, stage in stages:
                    o = s + ahead
                    if not isinstance(i, int) or 0 <= 2 * i + o <= NB:
                        stage(i + o // 2, o % 2)

            start = 1 + (behind + 1) // 2
            end = (NB - 2 - lead) // 2 + 1
            for n in range(-lead, 2 * start):
                step(n // 2, n % 2)
            with eng.Fori(start, end) as i:
                step(i, 0)
                step(i, 1)
            for n in range(2 * end, NB + 1 + behind):
                step(n // 2, n % 2)

        def put_before(eng, e, m, i, s):
            for q, (a, z) in enumerate(m.groups):
                eng.wait_ge(e.put_done[s][q], 16 * (z - a) * i)

        def put_all(eng, e, m):
            for s in range(2):
                for q, (a, z) in enumerate(m.groups):
                    eng.wait_ge(e.put_done[s][q], 16 * (z - a) * PAIRS + (16 if s == q == 0 else 0))

        def gathered(i, s):
            return 16 * G * i + 16 if short(i, s) else 16 * G * (i + 1)

        def entry_of(i, s, a, b):
            at = (2 * i + s) * ENTRY
            return plan[:, bass.ds(at + a, b - a)] if not isinstance(i, int) else plan[:, at + a:at + b]

        def edge_cols(a, i, s):
            at, n = (2 * i + s) * G, size(i, s)[0]
            return a[:, bass.ds(at, n)] if not isinstance(i, int) else a[:, at:at + n]

        def own(i, s):
            at, width = (2 * i + s) * G * D, size(i, s)[0] * D
            return nodes[:, bass.ds(at, width)] if not isinstance(i, int) else nodes[:, at:at + width]

        def window(first, w):
            return nodes[:, bass.ds(first * D, w * D)]

        CLEARS = 2 * (NB + 1)
        ENTRIES = 1

        block = ctx.enter_context(nc.Block())

        @block.sync
        def _(sp):
            reps = BLK // TAIL
            assert reps * TAIL == BLK
            for rows_1d, to, done in ((dst, tile_dst, s_dst), (src, tile_src, s_rows), (edge_weight, tile_w, s_rows)):
                sp.dma_start(to[0:NB, :], rows_1d[0:NB * BLK].rearrange("(b n) -> b n", n=BLK)).then_inc(done, 16)
                sp.dma_start(to[NB:NB + 1, :].rearrange("o (r n) -> o r n", r=reps),
                             rows_1d[NB * BLK:N].rearrange("(o r n) -> o r n", o=1, r=1)
                             .to_broadcast([1, reps, TAIL])).then_inc(done, 16)
            sp.dma_start(we[0:D, :], w_edge_t).then_inc(s_wts, 16)
            sp.dma_start(we[D:D + 1, :], b_edge).then_inc(s_wts, 16)
            sp.dma_start(w1[:, :], w1_t).then_inc(s_wts, 16)
            sp.dma_start(w2[0:D, :], w2_t).then_inc(s_wts, 16)
            sp.dma_start(w2[D:D + 1, :], b2).then_inc(s_wts, 16)
            sp.dma_start(b1c[:, :], b1).then_inc(s_wts, 16)
            sp.dma_start(eps1[:, :], eps.to_broadcast([P, 1])).then_inc(s_wts, 16)
            sp.wait_ge(s_entry, ENTRIES)
            sp.dma_start(plan_dram, entry[0:NB + 1, :]).then_inc(s_plan_out, 16)
            sp.wait_ge(s_plan_out, 16)
            sp.dma_start(plan[:, :], plan_dram.rearrange("(o b) e -> o (b e)", o=1)
                         .to_broadcast([P, (NB + 1) * ENTRY])).then_inc(s_plan, 16)

            def load_keys(e, m, key_1d, key, i, s):
                tiles, rows = size(i, s)
                sp.dma_start(key_col[0:rows, s, 0:tiles], by_block(key, i, s)).then_inc(e.key_in[s], 16)
                sp.dma_start(m.key_row[0:rows, s, 0:tiles * rows], as_row(key_1d, i, s)).then_inc(e.key_in[s], 16)

            def general_load0(i, s):
                tiles, rows = size(i, s)
                if had(i, s, 2):
                    done = 2 * i + s - 1
                    sp.wait_ge(e0.attr_tp, done)
                    sp.wait_ge(e0.put_ready, done)
                    sp.sem_inc(s_sp_go, 1)
                    sp.wait_ge(e0.got_in[s], 16 * G * i)
                sp.dma_start(get_col[0:rows, s, 0:tiles], by_block(src_c, i, s)).then_inc(e0.get_in[s], 16)
                load_keys(e0, M, dst, dst_c, i, s)
                sp.dma_start(M.attr[0:rows, s, 0:tiles * D], by_block(edge_attr, i, s)).then_inc(e0.load_in[s], 16)

            def general_load1(i, s):
                tiles, rows = size(i, s)
                if had(i, s, 2):
                    done = 2 * i + s - 1
                    sp.wait_ge(e1.msg_ready, done)
                    sp.wait_ge(e1.put_ready, done)
                    sp.sem_inc(s_sp_go, 1)
                    sp.wait_ge(e1.got_in[s], 16 * G * i)
                sp.dma_start(get_col[0:rows, s, 0:tiles], by_block(dst_c, i, s)).then_inc(e1.get_in[s], 16)
                load_keys(e1, M, src, src_c, i, s)
                sp.dma_start(wgt[0:rows, s, 0:tiles], by_block(w_c, i, s)).then_inc(e1.load_in[s], 16)

            def general_nodes(i, s):
                tiles, rows = size(i, s)
                if had(i, s, 2):
                    sp.wait_ge(n0.y, 2 * i + s - 1)
                sp.dma_start(M.xin[0:rows, s, 0:tiles * D], by_block(x, i, s)).then_inc(n0.x_in[s], 16)
                sp.dma_start(M.ain[0:rows, s, 0:tiles * D], by_block(table[0], i, s)).then_inc(n0.x_in[s], 16)

            def general_end(i, s):
                tiles, rows = size(i, s)
                if had(i, s, 2):
                    sp.wait_ge(n1.res, 2 * i + s - 1)
                sp.dma_start(M.fin[0:rows, s, 0:tiles * D], by_block(table[1], i, s)).then_inc(n1.x_in[s], 16)

            def fast_load0(i, s):
                tiles, rows = size(i, s)
                if had(i, s, 2):
                    sp.wait_ge(e0.attr_tp, 2 * i + s - 1)
                sp.dma_start(F.attr[0:rows, s, 0:tiles * D].rearrange("p (g d) -> p g d", g=tiles),
                             by_tile(edge_attr, i, s)).then_inc(e0.load_in[s], 16)

            def fast_nodes(i, s):
                tiles, rows = size(i, s)
                if had(i, s, 2):
                    sp.wait_ge(n0.kept, 2 * i + s - 1)
                sp.dma_start(F.xin[0:rows, s, 0:tiles * D].rearrange("p (g d) -> p g d", g=tiles),
                             by_tile(x, i, s)).then_inc(n0.x_in[s], 16)

            def fast_load1(i, s):
                tiles, rows = size(i, s)
                if had(i, s, 2):
                    sp.wait_ge(e1.matched, 2 * i + s - 1)
                    sp.wait_ge(e1.hot, 10 * i + 5 * s - 5)
                sp.dma_start(F.key_row[0:rows, s, 0:tiles * rows], as_row(src, i, s)).then_inc(e1.key_in[s], 16)
                r = as_row(dst, i, s)
                if short(i, s):
                    r = dst.rearrange("(o n) -> o n", o=1)[:, NB * BLK:N].to_broadcast([P, TAIL])
                sp.dma_start(F.dst_row[:, s, 0:tiles * rows], r).then_inc(e1.load_in[s], 16)

            def fast_end(i, s):
                tiles, rows = size(i, s)
                if had(i, s, 2):
                    sp.wait_ge(n1.ab, 2 * i + s - 1)
                for k, buf in enumerate((F.ain, F.bin)):
                    sp.dma_start(buf[0:rows, s, 0:tiles * D].rearrange("p (g d) -> p g d", g=tiles),
                                 by_tile(table[k], i, s)).then_inc(n1.x_in[s], 16)

            sp.wait_ge(s_plan, 16)
            sp.wait_ge(s_span, 1)
            fits = sp.value_load(span_all[0:1, 0:1], min_val=0, max_val=NT)
            with sp.If(fits < WIDE):
                sp.wait_ge(s_cols, 3)
                steps(sp, (0, fast_load0))
                sp.wait_ge(e0.win_add, NB * G + 1)
                steps(sp, (0, fast_nodes))
                sp.wait_ge(n0.res, NB + 1)
                steps(sp, (0, fast_load1))
                put_all(sp, e1, F)
                steps(sp, (0, fast_end))
            with sp.Else():
                steps(sp, (0, general_load0))
                put_all(sp, e0, M)
                steps(sp, (0, general_nodes))
                sp.wait_ge(n0.res, NB + 1)
                steps(sp, (0, general_load1))
                put_all(sp, e1, M)
                steps(sp, (0, general_end))

        @block.gpsimd
        def _(pool):
            nc.gpsimd.memset(ident[:, :], 1.0).then_inc(s_const, 1)
            nc.gpsimd.memset(after[:, :], 1.0).then_inc(s_const, 1)
            nc.gpsimd.iota(number_i[:, :], pattern=[[P, G]], base=0, channel_multiplier=1).then_inc(s_iota, 1)
            nc.gpsimd.iota(count_i, pattern=[[1, WIDE * P]], base=0, channel_multiplier=0).then_inc(s_iota, 1)
            pool.wait_ge(s_const, 2)
            nc.gpsimd.affine_select(out=ident[:, :], in_=ident[:, :], compare_op=ALU.is_equal, fill=0.0,
                                    base=0, pattern=[[-1, P]], channel_multiplier=1).then_inc(s_const, 1)
            nc.gpsimd.affine_select(out=after[:, :], in_=after[:, :], compare_op=ALU.is_ge, fill=0.0,
                                    base=0, pattern=[[1, BLK]], channel_multiplier=-1).then_inc(s_const, 1)

            def gather(e, rows_of, to, i, s):
                tiles, rows = size(i, s)
                if to is F.got:
                    pool.wait_ge(s_get, 2 * i + s + 1)
                else:
                    pool.wait_ge(e.get_in[s], 16 * (i + 1))
                if had(i, s, 2):
                    pool.wait_ge(e.added if e is e0 else e.msg_ready, 2 * i + s - 1)
                pool.sem_inc(s_pool_go, 1)
                for g in range(tiles):
                    nc.gpsimd.indirect_dma_start(
                        to[0:rows, s, g * D:(g + 1) * D], None, rows_of,
                        bass.IndirectOffsetOnAxis(ap=get_col[0:rows, s, g:g + 1], axis=0),
                    ).then_inc(e.got_in[s], 16)

            def scatter(e, m, into, i, s):
                tiles, rows = size(i, s)
                for q, (a, z) in enumerate(m.groups):
                    if a >= tiles:
                        continue
                    pool.wait_ge(s_cleared, 16 * CLEARS)
                    if had(i, s, 1):
                        pool.wait_ge(e.put_done[1 - s][q], 16 * (z - a) * (i + s))
                    pool.wait_ge(e.put_ready, 2 * i + s + 1)
                    pool.wait_ge(e.sums_ready, 2 * i + s + 1)
                    pool.sem_inc(s_pool_go, 1)
                    for g in range(a, min(z, tiles)):
                        nc.gpsimd.indirect_dma_start(
                            into[q], bass.IndirectOffsetOnAxis(ap=put_col[0:rows, s, g:g + 1], axis=0),
                            m.sums[0:rows, s, g * D:(g + 1) * D], None, compute_op=ALU.add,
                        ).then_inc(e.put_done[s][q], 16)

            def keep_x(i, s):
                tiles, rows = size(i, s)
                pool.wait_ge(n0.h, 2 * i + s + 1)
                nc.gpsimd.tensor_copy(own(i, s)[0:rows, :], F.xin[0:rows, s, 0:tiles * D]).then_inc(n0.kept, 1)

            def add_tables(i, s):
                tiles, rows = size(i, s)
                pool.wait_ge(n1.x_in[s], 32 * (i + 1))
                if had(i, s, 2):
                    pool.wait_ge(n1.y, 2 * i + s - 1)
                nc.gpsimd.tensor_tensor(F.ab[0:rows, s, 0:tiles * D], F.ain[0:rows, s, 0:tiles * D],
                                        F.bin[0:rows, s, 0:tiles * D], ALU.add).then_inc(n1.ab, 1)

            pool.wait_ge(s_span, 1)
            fits = pool.value_load(span_all[0:1, 0:1], min_val=0, max_val=NT)
            with pool.If(fits < WIDE):
                steps(pool, (0, lambda *b: gather(e0, x, F.got, *b)))
                steps(pool, (0, keep_x))
                steps(pool, (0, lambda *b: scatter(e1, F, table, *b)))
                steps(pool, (0, add_tables))
            with pool.Else():
                steps(pool, (1, lambda *b: gather(e0, x, M.got, *b)), (0, lambda *b: scatter(e0, M, (table[0],), *b)))
                pool.wait_ge(n0.stored[1], 32 * PAIRS)
                pool.wait_ge(n0.stored[0], 32 * PAIRS + 32)
                steps(pool, (1, lambda *b: gather(e1, h_dram, M.got, *b)), (0, lambda *b: scatter(e1, M, (table[1],), *b)))

        @block.scalar
        def _(act):
            def clear(i, s):
                for t in table:
                    if short(i, s):
                        rest = (N + SPARE - NB * BLK) * D
                        act.dma_start(t[NB * BLK:N + SPARE, :].rearrange("n d -> (n d)").rearrange("(p w) -> p w", p=P),
                                      zeros[:, 0:rest // P]).then_inc(s_cleared, 16)
                    else:
                        act.dma_start(by_block(t, i, s), zeros[:, 0:G * D]).then_inc(s_cleared, 16)

            def attr_to_sbuf(i, s):
                tiles, rows = size(i, s)
                m = (tiles - 1) * P + rows
                act.wait_ge(e0.attr_tp, 2 * i + s + 1)
                if had(i, s, 2):
                    act.wait_ge(e0.ea_mm, 2 * i + s - 1)
                nc.scalar.copy(attr_t[s][0:D, 0:m], wide[s][0:D, 0:m]).then_inc(e0.attr_ts, 1)

            def sums_to_sbuf(e, m, i, s):
                tiles, rows = size(i, s)
                act.wait_ge(e.sum_mm, 2 * i + s + 1)
                if had(i, s, 2):
                    put_before(act, e, m, i, s)
                nc.scalar.copy(m.sums[0:rows, s, 0:tiles * D], tot_ps[s][0:rows, 0:tiles * D]).then_inc(e.sums_ready, 1)

            def messages0(m, i, s):
                tiles, rows = size(i, s)
                act.wait_ge(e0.added, 2 * i + s + 1)
                if had(i, s, 2):
                    if m is F:
                        act.wait_ge(e0.win_mm, 10 * i + 5 * s - 5)
                    else:
                        act.wait_ge(e0.sum_mm, 2 * i + s - 1)
                nc.scalar.activation(m.msg[0:rows, s, 0:tiles * D], m.pre[0:rows, s, 0:tiles * D],
                                     ACT.Relu).then_inc(e0.msg_ready, 1)

            def messages1(i, s):
                tiles, rows = size(i, s)
                act.wait_ge(e1.win_mm, 10 * i + 5 * s + tiles)
                if had(i, s, 2):
                    act.wait_ge(e1.sum_mm, 2 * i + s - 1)
                for g in range(tiles):
                    ins = nc.scalar.activation(F.msg1[0:rows, s, g * D:(g + 1) * D], mid[s][0:rows, g * D:(g + 1) * D],
                                               ACT.Copy, scale=edge_cols(w_col, i, s)[0:rows, g:g + 1])
                ins.then_inc(e1.msg_ready, 1)

            def turned_to_sbuf(i, s):
                tiles, rows = size(i, s)
                m = (tiles - 1) * P + rows
                act.wait_ge(n0.tp, 2 * i + s + 1)
                if had(i, s, 1):
                    act.wait_ge(n0.hid_mm, 2 * i + s)
                nc.scalar.copy(h_t[:, 0:m], wide[0][0:D, 0:m]).then_inc(n0.ts, 1)

            def hidden_to_sbuf(i, s):
                tiles, rows = size(i, s)
                m = (tiles - 1) * P + rows
                act.wait_ge(n0.hid_mm, 2 * i + s + 1)
                if had(i, s, 2):
                    act.wait_ge(n0.out_mm, 2 * i + s - 1)
                nc.scalar.activation(hid_t[s][0:D, 0:m], wide[1][0:D, 0:m], ACT.Relu,
                                     bias=b1c[:, 0:1]).then_inc(n0.hid, 1)

            def root(n, i, s):
                tiles, rows = size(i, s)
                act.wait_ge(n.mv, 2 * i + s + 1)
                if had(i, s, 2):
                    act.wait_ge(n.rstd, 2 * i + s - 1)
                nc.scalar.activation(std[0:rows, s, 0:tiles],
                                     mv[0:rows, s, 0:2 * tiles].rearrange("p (g k) -> p g k", k=2)[:, :, 1],
                                     ACT.Sqrt, bias=lneps[0:rows, 0:1]).then_inc(n.std, 1)

            def normalize(n, y, to, i, s):
                tiles, rows = size(i, s)
                act.wait_ge(n.shift, 2 * i + s + 1)
                for g in range(tiles):
                    ins = nc.scalar.activation(to[0:rows, g * D:(g + 1) * D], y[0:rows, s, g * D:(g + 1) * D],
                                               ACT.Identity, scale=rstd[0:rows, s, g:g + 1],
                                               bias=shift[0:rows, s, g:g + 1])
                ins.then_inc(n.res, 1)

            def end(m, y, tiled, i, s):
                if had(i, s, 2):
                    act.wait_ge(n1.stored[s], 16 * i)
                normalize(n1, y, m.res[:, s, :], i, s)
                store(n1, m.res, (out,), tiled, i, s)

            def end0(i, s):
                if had(i, s, 2):
                    act.wait_ge(n0.stored[s], 32 * i)
                normalize(n0, M.y, M.res[:, s, :], i, s)
                store(n0, M.res, (h_dram, table[1][0:N, :]), False, i, s)

            def store(n, res, tables, tiled, i, s):
                tiles, rows = size(i, s)
                act.wait_ge(n.res, 2 * i + s + 1)
                for t in tables:
                    if tiled:
                        act.dma_start(by_tile(t, i, s), res[0:rows, s, 0:tiles * D]
                                      .rearrange("p (g d) -> p g d", g=tiles)).then_inc(n.stored[s], 16)
                    else:
                        act.dma_start(by_block(t, i, s), res[0:rows, s, 0:tiles * D]).then_inc(n.stored[s], 16)

            act.wait_ge(s_eps, 1)
            act.wait_ge(s_zero, 1)
            act.wait_ge(s_span, 1)
            fits = act.value_load(span_all[0:1, 0:1], min_val=0, max_val=NT)
            half = NT // 2 * D
            with act.If(fits < WIDE):
                nc.scalar.activation(nodes[:, half:NT * D].rearrange("p (r w) -> p r w", w=D),
                                     zeros[:, 0:D].unsqueeze(1).to_broadcast([P, (NT * D - half) // D, D]),
                                     ACT.Copy).then_inc(s_nodes0, 1)
                steps(act, (3, attr_to_sbuf), (1, lambda *b: messages0(F, *b)), (0, clear))
                steps(act, (1, hidden_to_sbuf), (2, turned_to_sbuf), (0, lambda *b: root(n0, *b)),
                      (-1, lambda *b: normalize(n0, F.y, own(*b), *b)))
                steps(act, (0, messages1), (-1, lambda *b: sums_to_sbuf(e1, F, *b)))
                steps(act, (1, lambda *b: root(n1, *b)), (0, lambda *b: end(F, F.yf, True, *b)))
            with act.Else():
                steps(act, (0, clear))
                steps(act, (1, attr_to_sbuf), (0, lambda *b: messages0(M, *b)), (0, lambda *b: sums_to_sbuf(e0, M, *b)))
                steps(act, (1, turned_to_sbuf), (1, hidden_to_sbuf), (0, lambda *b: root(n0, *b)), (-1, end0))
                steps(act, (0, lambda *b: sums_to_sbuf(e1, M, *b)))
                steps(act, (1, lambda *b: root(n1, *b)), (0, lambda *b: end(M, M.fin, False, *b)))
            act.wait_ge(n1.stored[1], 16 * PAIRS)
            act.wait_ge(n1.stored[0], 16 * PAIRS + 16)

        @block.vector
        def _(dve):
            nc.vector.memset(zeros[:, :], 0.0).then_inc(s_zero, 1)
            nc.vector.memset(attr_t[0][D:D + 1, :], 1.0).then_inc(s_ones, 1)
            nc.vector.memset(attr_t[1][D:D + 1, :], 1.0).then_inc(s_ones, 1)
            nc.vector.memset(lneps[:, :], LN_EPS).then_inc(s_eps, 1)
            nc.vector.memset(entry[0:NB + 1, :], 0).then_inc(s_step, 1)

            dve.wait_ge(s_dst, 32)
            cut = tile_dst[0:NB + 1, :].rearrange("b (g n) -> b g n", g=G)
            nc.vector.tensor_reduce(out=least[0:NB + 1, :], in_=cut, axis=mybir.AxisListType.X, op=ALU.min).then_inc(s_step, 1)
            nc.vector.tensor_reduce(out=most[0:NB + 1, :], in_=cut, axis=mybir.AxisListType.X, op=ALU.max).then_inc(s_step, 1)
            dve.wait_ge(s_step, 3)
            nc.vector.tensor_copy(least_i[0:NB + 1, :], least[0:NB + 1, :]).then_inc(s_step, 1)
            nc.vector.tensor_copy(most_i[0:NB + 1, :], most[0:NB + 1, :]).then_inc(s_step, 1)
            dve.wait_ge(s_step, 5)
            nc.vector.tensor_scalar(first_i[0:NB + 1, :], least_i[0:NB + 1, :], 7, None, ALU.arith_shift_right).then_inc(s_step, 1)
            nc.vector.tensor_scalar(end_i[0:NB + 1, :], most_i[0:NB + 1, :], 7, None, ALU.arith_shift_right).then_inc(s_step, 1)
            dve.wait_ge(s_step, 7)
            nc.vector.tensor_scalar(entry[0:NB + 1, 0:G], first_i[0:NB + 1, :], NT - WIDE, None, ALU.min).then_inc(s_step, 1)
            dve.wait_ge(s_step, 8)
            nc.vector.tensor_tensor(spans[0:NB + 1, :], end_i[0:NB + 1, :], entry[0:NB + 1, 0:G], ALU.subtract).then_inc(s_step, 1)
            dve.wait_ge(s_step, 9)
            nc.vector.tensor_reduce(out=entry[0:NB + 1, SPAN:SPAN + 1], in_=spans[0:NB + 1, :],
                                    axis=mybir.AxisListType.X, op=ALU.max).then_inc(s_entry, 1)

            dve.wait_ge(s_iota, 2)
            nc.vector.tensor_copy(window_row[:, :], number_i[:, 0:WIDE]).then_inc(s_number, 1)
            nc.vector.tensor_scalar(spare_row[:, :], number_i[:, 0:G], float(N), None, ALU.add).then_inc(s_number, 1)
            nc.vector.tensor_copy(count_up[:, :], count_i).then_inc(s_number, 1)
            dve.wait_ge(s_wts, 16 * 7)
            nc.vector.tensor_scalar(eps1[:, :], eps1[:, :], 1.0, None, ALU.add).then_inc(s_number, 1)
            dve.wait_ge(s_number, 4)
            dve.wait_ge(s_const, 4)
            dve.wait_ge(s_plan, 16)
            nc.vector.tensor_reduce(out=span_all[0:1, 0:1],
                                    in_=plan[0:1, :].rearrange("o (b e) -> o b e", e=ENTRY)[:, :, SPAN],
                                    axis=mybir.AxisListType.X, op=ALU.max).then_inc(s_span, 1)

            def match(e, m, tiled, i, s):
                tiles, rows = size(i, s)
                dve.wait_ge(e.key_in[s], (16 if tiled else 32) * (i + 1))
                if had(i, s, 2):
                    dve.wait_ge(e.sum_mm, 2 * i + s - 1)
                own_key = edge_cols(src_col, i, s) if tiled else key_col[:, s, 0:tiles]
                keys = m.key_row[0:rows, s, 0:tiles * rows]
                by_g = keys.rearrange("k (g p) -> k g p" if tiled else "k (p g) -> k g p", g=tiles)
                for g in range(tiles):
                    end_ = min(tiles, next(z for a, z in m.groups if a <= g < z))
                    n = end_ - g
                    out_ = m.same[0:rows, s, m.tri[g, g]:m.tri[g, g] + (n - 1) * P + rows]
                    ins = nc.vector.scalar_tensor_tensor(
                        out=out_.rearrange("k (g p) -> k g p", g=n),
                        in0=by_g[:, g:end_, :], scalar=own_key[0:rows, g:g + 1],
                        in1=after[0:rows, 0:(n - 1) * P + rows].rearrange("k (g p) -> k g p", g=n),
                        op0=ALU.is_equal, op1=ALU.mult, accum_out=count[0:rows, s, g:g + 1])
                ins.then_inc(e.matched, 1)
                nc.vector.tensor_tensor(off_spare[0:rows, s, 0:tiles], own_key[0:rows, :],
                                        spare_row[0:rows, 0:tiles], ALU.subtract)
                dve.wait_ge(e.matched, 2 * i + s + 1)
                nc.vector.tensor_scalar(is_last[0:rows, s, 0:tiles], count[0:rows, s, 0:tiles], 1.0, None,
                                        ALU.is_equal).then_inc(e.dve, 1)
                dve.wait_ge(e.dve, 4 * i + 2 * s + 1)
                nc.vector.tensor_tensor(off_last[0:rows, s, 0:tiles], off_spare[0:rows, s, 0:tiles],
                                        is_last[0:rows, s, 0:tiles], ALU.mult).then_inc(e.dve, 1)

            def aim(e, m, i, s):
                tiles, rows = size(i, s)
                dve.wait_ge(e.dve, 4 * i + 2 * s + 2)
                if had(i, s, 2):
                    put_before(dve, e, m, i, s)
                nc.vector.tensor_tensor(put_col[0:rows, s, 0:tiles], off_last[0:rows, s, 0:tiles],
                                        spare_row[0:rows, 0:tiles], ALU.add).then_inc(e.put_ready, 1)

            def add_x(m, i, s):
                tiles, rows = size(i, s)
                dve.wait_ge(e0.ea_mm, 2 * i + s + 1)
                dve.wait_ge(e0.got_in[s], gathered(i, s))
                if had(i, s, 2):
                    dve.wait_ge(e0.msg_ready, 2 * i + s - 1)
                nc.vector.tensor_tensor(m.pre[0:rows, s, 0:tiles * D], mid[s][0:rows, 0:tiles * D],
                                        m.got[0:rows, s, 0:tiles * D], ALU.add).then_inc(e0.added, 1)

            def to_columns():
                dve.wait_ge(s_rows, 64)
                nc.vector.tensor_copy(tile_f[0:NB + 1, 0:BLK], tile_dst[0:NB + 1, :]).then_inc(s_float, 1)
                nc.vector.tensor_copy(tile_f[0:NB + 1, BLK:2 * BLK], tile_src[0:NB + 1, :]).then_inc(s_float, 1)
                for k, to in enumerate((dst_col, src_col, w_col)):
                    dve.wait_ge(s_turned, k + 1)
                    nc.vector.tensor_copy(to[:, :].rearrange("p (b g) -> p g b", g=G),
                                          wide[k % 2][:, 0:G * P].rearrange("p (g b) -> p g b", g=G)[:, :, 0:NB + 1]
                                          ).then_inc(s_cols, 1)
                dve.wait_ge(s_cols, 3)

            def get_rows(i, s):
                tiles, rows = size(i, s)
                if had(i, s, 2):
                    dve.wait_ge(e0.got_in[s], 16 * G * i)
                nc.vector.tensor_copy(get_col[0:rows, s, 0:tiles], edge_cols(src_col, i, s)[0:rows, :]).then_inc(s_get, 1)

            def windows_of(i, s):
                at = entry_of(i, s, 0, ENTRY)
                _, v = nc.values_load_multi_w_load_instructions(
                    at[0:1, 0:SPAN + 1], engines=(ENG.DVE,), min_val=0, max_val=NT - WIDE,
                    skip_runtime_bounds_check_because="the plan holds windows inside the nodes")
                return v[0:G], v[SPAN]

            def locate(i, s):
                tiles, rows = size(i, s)
                if had(i, s, 2):
                    dve.wait_ge(e0.hot, 10 * i + 5 * s - 5)
                nc.vector.scalar_tensor_tensor(
                    out=local[0:rows, s, 0:tiles], in0=entry_of(i, s, 0, tiles)[0:rows, :], scalar=-float(P),
                    in1=edge_cols(dst_col, i, s)[0:rows, :], op0=ALU.mult, op1=ALU.add).then_inc(e0.local, 1)
                dve.wait_ge(e0.local, 2 * i + s + 1)

            def mark(i, s, g):
                rows = size(i, s)[1]
                if had(i, s, 1):
                    dve.wait_ge(e0.win_mm, 10 * i + 5 * s + g - 4)
                nc.vector.tensor_scalar(hot[0:rows, g, :], count_up[0:rows, :], local[0:rows, s, g:g + 1], None,
                                        ALU.is_equal).then_inc(e0.hot, 1)

            def window_sums(i, s):
                tiles, rows = size(i, s)
                after_i, after_s = i + (s + 1) // 2, (s + 1) % 2
                ahead = 0 if short(i, s) else size(after_i, after_s)[0]
                first, span = windows_of(i, s)
                if ahead:
                    locate(after_i, after_s)
                dve.sem_inc(s_dve_go, 1)

                def by_width(w):
                    for g in range(tiles):
                        t = 10 * i + 5 * s + g
                        dve.wait_ge(e0.win_mm, t + 1)
                        if had(i, s, 1) or g >= 1:
                            dve.wait_ge(e0.win_add, t)
                        nc.vector.tensor_tensor(window(first[g], w), window(first[g], w),
                                                tot_ps[(s + g) % 2][:, 0:w * D], ALU.add).then_inc(e0.win_add, 1)
                        if g < ahead:
                            mark(after_i, after_s, g)

                with dve.If(span < NARROW):
                    by_width(NARROW)
                with dve.Else():
                    by_width(WIDE)

            def form_h(m, i, s):
                tiles, rows = size(i, s)
                dve.wait_ge(n0.x_in[s], (32 if m is M else 16) * (i + 1))
                if had(i, s, 2):
                    dve.wait_ge(n0.tp, 2 * i + s - 1)
                sums = m.ain[0:rows, s, 0:tiles * D] if m is M else own(i, s)[0:rows, :]
                nc.vector.scalar_tensor_tensor(
                    out=m.hin[0:rows, s, 0:tiles * D], in0=m.xin[0:rows, s, 0:tiles * D], scalar=eps1[0:rows, 0:1],
                    in1=sums, op0=ALU.mult, op1=ALU.add).then_inc(n0.h, 1)

            def residual(m, i, s):
                tiles, rows = size(i, s)
                dve.wait_ge(n0.out_mm, 2 * i + s + 1)
                if had(i, s, 2):
                    dve.wait_ge(n0.res, 2 * i + s - 1)
                if m is F:
                    dve.wait_ge(n0.kept, 2 * i + s + 1)
                x_in = m.xin[0:rows, s, 0:tiles * D] if m is M else own(i, s)[0:rows, :]
                nc.vector.tensor_tensor(m.y[0:rows, s, 0:tiles * D], mid[s][0:rows, 0:tiles * D],
                                        x_in, ALU.add).then_inc(n0.y, 1)

            def statistics(n, y, i, s):
                tiles, rows = size(i, s)
                for g in range(tiles):
                    ins = nc.vector.bn_stats(out=stats[0:rows, s, 6 * g:6 * g + 6], in_=y[0:rows, s, g * D:(g + 1) * D])
                ins.then_inc(n.stats, 1)
                dve.wait_ge(n.stats, 2 * i + s + 1)
                if had(i, s, 2):
                    dve.wait_ge(n.shift, 2 * i + s - 1)
                dve.sem_inc(s_dve_go, 1)
                for g in range(tiles):
                    ins = nc.vector.bn_aggr(out=mv[0:rows, s, 2 * g:2 * g + 2], in_=stats[0:rows, s, 6 * g:6 * g + 6])
                ins.then_inc(n.mv, 1)

            def scales(n, i, s):
                tiles, rows = size(i, s)
                dve.wait_ge(n.std, 2 * i + s + 1)
                if had(i, s, 2):
                    dve.wait_ge(n.res, 2 * i + s - 1)
                nc.vector.reciprocal(rstd[0:rows, s, 0:tiles], std[0:rows, s, 0:tiles]).then_inc(n.rstd, 1)
                dve.wait_ge(n.rstd, 2 * i + s + 1)
                nc.vector.scalar_tensor_tensor(
                    out=shift[0:rows, s, 0:tiles], in0=mv[0:rows, s, 0:2 * tiles].rearrange("p (g k) -> p g k", k=2)[:, :, 0],
                    scalar=-1.0, in1=rstd[0:rows, s, 0:tiles], op0=ALU.mult, op1=ALU.mult).then_inc(n.shift, 1)

            def layer0_block(m, i, s):
                residual(m, i, s)
                dve.wait_ge(n0.y, 2 * i + s + 1)
                statistics(n0, m.y, i, s)

            def weigh(i, s):
                tiles, rows = size(i, s)
                dve.wait_ge(e1.load_in[s], 16 * (i + 1))
                dve.wait_ge(e1.got_in[s], gathered(i, s))
                if had(i, s, 2):
                    dve.wait_ge(e1.sum_mm, 2 * i + s - 1)
                cut3 = lambda a: a[0:rows, s, 0:tiles * D].rearrange("p (g d) -> p g d", g=tiles)
                nc.vector.tensor_tensor(cut3(M.msg), cut3(M.got),
                                        wgt[0:rows, s, 0:tiles].unsqueeze(2).to_broadcast([rows, tiles, D]),
                                        ALU.mult).then_inc(e1.msg_ready, 1)

            def window_marks(i, s):
                tiles, rows = size(i, s)
                _, (span,) = nc.values_load_multi_w_load_instructions(
                    entry_of(i, s, SPAN, SPAN + 1)[0:1, :], engines=(ENG.DVE,), min_val=0, max_val=NT,
                    skip_runtime_bounds_check_because="it only picks the window's width")
                if had(i, s, 2):
                    dve.wait_ge(e1.hot, 10 * i + 5 * s - 5)
                spread = lambda a: a.unsqueeze(2).to_broadcast([P, tiles, WIDE])
                nc.vector.scalar_tensor_tensor(
                    out=local_row[:, s, 0:tiles * WIDE].rearrange("p (g j) -> p g j", g=tiles),
                    in0=spread(entry_of(i, s, 0, tiles)), scalar=float(P),
                    in1=window_row[:, :].unsqueeze(1).to_broadcast([P, tiles, WIDE]),
                    op0=ALU.mult, op1=ALU.add).then_inc(e1.local, 1)
                dve.wait_ge(e1.local, 2 * i + s + 1)
                dve.wait_ge(e1.load_in[s], 16 * (i + 1))
                dve.sem_inc(s_dve_go, 1)

                def by_width(w):
                    for g in range(tiles):
                        if had(i, s, 1):
                            dve.wait_ge(e1.win_mm, 10 * i + 5 * s + g - 4)
                        nc.vector.tensor_tensor(
                            hot[:, g, 0:w * P].rearrange("p (j e) -> p j e", j=w)[:, :, 0:rows],
                            F.dst_row[:, s, g * P:g * P + rows].unsqueeze(1).to_broadcast([P, w, rows]),
                            local_row[:, s, WIDE * g:WIDE * g + w].unsqueeze(2).to_broadcast([P, w, rows]),
                            ALU.is_equal).then_inc(e1.hot, 1)

                with dve.If(span < NARROW):
                    by_width(NARROW)
                with dve.Else():
                    by_width(WIDE)

            def add_h(i, s):
                tiles, rows = size(i, s)
                dve.wait_ge(n1.ab, 2 * i + s + 1)
                if had(i, s, 2):
                    dve.wait_ge(n1.res, 2 * i + s - 1)
                nc.vector.tensor_tensor(F.yf[0:rows, s, 0:tiles * D], F.ab[0:rows, s, 0:tiles * D],
                                        own(i, s)[0:rows, :], ALU.add).then_inc(n1.y, 1)
                dve.wait_ge(n1.y, 2 * i + s + 1)
                statistics(n1, F.yf, i, s)

            def general_statistics(i, s):
                dve.wait_ge(n1.x_in[s], 16 * (i + 1))
                statistics(n1, M.fin, i, s)

            dve.wait_ge(s_span, 1)
            fits = dve.value_load(span_all[0:1, 0:1], min_val=0, max_val=NT)
            half = NT // 2 * D
            with dve.If(fits < WIDE):
                to_columns()
                nc.vector.memset(nodes[:, 0:half], 0.0).then_inc(s_nodes0, 1)
                dve.wait_ge(s_nodes0, 2)
                locate(0, 0)
                for g in range(G):
                    mark(0, 0, g)
                steps(dve, (2, get_rows), (1, lambda *b: add_x(F, *b)), (0, window_sums))
                dve.wait_ge(e0.win_add, NB * G + 1)
                steps(dve, (2, lambda *b: form_h(F, *b)), (-1, lambda *b: scales(n0, *b)),
                      (0, lambda *b: layer0_block(F, *b)))
                dve.wait_ge(n0.res, NB + 1)
                steps(dve, (1, window_marks), (1, lambda *b: match(e1, F, True, *b)), (0, lambda *b: aim(e1, F, *b)))
                steps(dve, (1, add_h), (0, lambda *b: scales(n1, *b)))
            with dve.Else():
                steps(dve, (1, lambda *b: match(e0, M, False, *b)), (0, lambda *b: add_x(M, *b)),
                      (0, lambda *b: aim(e0, M, *b)))
                steps(dve, (1, lambda *b: form_h(M, *b)), (0, lambda *b: layer0_block(M, *b)),
                      (-1, lambda *b: scales(n0, *b)))
                steps(dve, (1, lambda *b: match(e1, M, False, *b)), (0, weigh), (0, lambda *b: aim(e1, M, *b)))
                steps(dve, (1, general_statistics), (0, lambda *b: scales(n1, *b)))

        @block.tensor
        def _(pe):
            pe.wait_ge(s_const, 4)
            pe.wait_ge(s_wts, 16 * 7)
            pe.wait_ge(s_ones, 2)

            def turn_attr(m, i, s):
                tiles, rows = size(i, s)
                pe.wait_ge(e0.load_in[s], 16 * (i + 1))
                if had(i, s, 2):
                    pe.wait_ge(e0.attr_ts, 2 * i + s - 1)
                for g in range(tiles):
                    ins = nc.tensor.transpose(wide[s][0:D, g * P:g * P + rows], m.attr[0:rows, s, g * D:(g + 1) * D],
                                              ident[0:rows, 0:rows])
                ins.then_inc(e0.attr_tp, 1)

            def edge_linear(i, s):
                tiles, rows = size(i, s)
                pe.wait_ge(e0.attr_ts, 2 * i + s + 1)
                if had(i, s, 2):
                    pe.wait_ge(e0.added, 2 * i + s - 1)
                for g in range(tiles):
                    ins = nc.tensor.matmul(mid[s][0:rows, g * D:(g + 1) * D], attr_t[s][:, g * P:g * P + rows],
                                           we[:, :], start=True, stop=True)
                ins.then_inc(e0.ea_mm, 1)

            def window_products(i, s):
                tiles, rows = size(i, s)
                _, (span,) = nc.values_load_multi_w_load_instructions(
                    entry_of(i, s, SPAN, SPAN + 1)[0:1, :], engines=(ENG.PE,), min_val=0, max_val=NT,
                    skip_runtime_bounds_check_because="it only picks the window's width")
                pe.wait_ge(e0.msg_ready, 2 * i + s + 1)

                def by_width(w):
                    for g in range(tiles):
                        t = 10 * i + 5 * s + g
                        pe.wait_ge(e0.hot, t + 1)
                        if had(i, s, 1) or g >= 2:
                            pe.wait_ge(e0.win_add, t - 1)
                        k = (s + g) % 2
                        for j in range(w):
                            ins = nc.tensor.matmul(tot_ps[k][:, j * D:(j + 1) * D], hot[0:rows, g, j * P:(j + 1) * P],
                                                   F.msg[0:rows, s, g * D:(g + 1) * D], start=True, stop=True)
                        ins.then_inc(e0.win_mm, 1)

                with pe.If(span < NARROW):
                    by_width(NARROW)
                with pe.Else():
                    by_width(WIDE)

            def window_gather(i, s):
                tiles, rows = size(i, s)
                _, v = nc.values_load_multi_w_load_instructions(
                    entry_of(i, s, 0, SPAN + 1)[0:1, :], engines=(ENG.PE,), min_val=0, max_val=NT - WIDE,
                    skip_runtime_bounds_check_because="the plan holds windows inside the nodes")
                first, span = v[0:G], v[SPAN]
                if had(i, s, 2):
                    pe.wait_ge(e1.msg_ready, 2 * i + s - 1)

                def by_width(w):
                    for g in range(tiles):
                        pe.wait_ge(e1.hot, 10 * i + 5 * s + g + 1)
                        for j in range(w):
                            ins = nc.tensor.matmul(mid[s][0:rows, g * D:(g + 1) * D], hot[:, g, j * P:j * P + rows],
                                                   nodes[:, bass.ds(first[g] * D + j * D, D)],
                                                   start=(j == 0), stop=(j == w - 1))
                        ins.then_inc(e1.win_mm, 1)

                with pe.If(span < NARROW):
                    by_width(NARROW)
                with pe.Else():
                    by_width(WIDE)

            def block_sums(e, m, i, s):
                tiles, rows = size(i, s)
                pe.wait_ge(e.matched, 2 * i + s + 1)
                pe.wait_ge(e.msg_ready, 2 * i + s + 1)
                if had(i, s, 2):
                    pe.wait_ge(e.sums_ready, 2 * i + s - 1)
                for g in range(tiles):
                    first = next(a for a, z in m.groups if a <= g < z)
                    for k in range(first, g + 1):
                        ins = nc.tensor.matmul(tot_ps[s][0:rows, g * D:(g + 1) * D],
                                               m.same[0:rows, s, m.tri[k, g]:m.tri[k, g] + rows],
                                               m.msg1[0:rows, s, k * D:(k + 1) * D], start=(k == first), stop=(k == g))
                ins.then_inc(e.sum_mm, 1)

            def turn_h(m, i, s):
                tiles, rows = size(i, s)
                pe.wait_ge(n0.h, 2 * i + s + 1)
                if had(i, s, 1):
                    pe.wait_ge(n0.ts, 2 * i + s)
                for g in range(tiles):
                    ins = nc.tensor.transpose(wide[0][0:D, g * P:g * P + rows], m.hin[0:rows, s, g * D:(g + 1) * D],
                                              ident[0:rows, 0:rows])
                ins.then_inc(n0.tp, 1)

            def hidden(i, s):
                tiles, rows = size(i, s)
                n = (tiles - 1) * P + rows
                pe.wait_ge(n0.ts, 2 * i + s + 1)
                if had(i, s, 1):
                    pe.wait_ge(n0.hid, 2 * i + s)
                for at in range(0, n, BANK):
                    to = min(n, at + BANK)
                    ins = nc.tensor.matmul(wide[1][0:D, at:to], w1[:, :], h_t[:, at:to], start=True, stop=True)
                ins.then_inc(n0.hid_mm, 1)

            def project(i, s):
                tiles, rows = size(i, s)
                pe.wait_ge(n0.hid, 2 * i + s + 1)
                if had(i, s, 2):
                    pe.wait_ge(n0.y, 2 * i + s - 1)
                for g in range(tiles):
                    ins = nc.tensor.matmul(mid[s][0:rows, g * D:(g + 1) * D], hid_t[s][:, g * P:g * P + rows],
                                           w2[:, :], start=True, stop=True)
                ins.then_inc(n0.out_mm, 1)

            pe.wait_ge(s_plan, 16)
            pe.wait_ge(s_span, 1)
            fits = pe.value_load(span_all[0:1, 0:1], min_val=0, max_val=NT)
            with pe.If(fits < WIDE):
                pe.wait_ge(s_float, 2)
                pe.wait_ge(s_rows, 64)
                for k, rows_f in enumerate((tile_f[:, 0:BLK], tile_f[:, BLK:2 * BLK], tile_w)):
                    if k == 2:
                        pe.wait_ge(s_cols, 1)
                    for g in range(G):
                        ins = nc.tensor.transpose(wide[k % 2][:, g * P:g * P + NB + 1],
                                                  rows_f[0:NB + 1, g * P:(g + 1) * P], ident[0:NB + 1, 0:NB + 1])
                    ins.then_inc(s_turned, 1)
                pe.wait_ge(s_cols, 3)
                steps(pe, (3, lambda *b: turn_attr(F, *b)), (2, edge_linear), (0, window_products))
                steps(pe, (1, hidden), (0, project), (2, lambda *b: turn_h(F, *b)))
                pe.wait_ge(n0.res, NB + 1)
                steps(pe, (0, window_gather), (-1, lambda *b: block_sums(e1, F, *b)))
            with pe.Else():
                steps(pe, (1, lambda *b: turn_attr(M, *b)), (1, edge_linear), (0, lambda *b: block_sums(e0, M, *b)))
                steps(pe, (1, lambda *b: turn_h(M, *b)), (1, hidden), (0, project))
                steps(pe, (0, lambda *b: block_sums(e1, M, *b)))


def kernel(x, src, dst, edge_attr_96, edge_weight, L0_gnn_W_edge, L0_gnn_b_edge, L0_gnn_eps, L0_gnn_W1, L0_gnn_b1,
           L0_gnn_W2, L0_gnn_b2):
    import numpy as np
    import concourse.bacc as bacc
    from concourse import mybir as mb
    from concourse.bass_utils import run_bass_kernel_spmd

    laid_out = {
        "x": x, "src": src, "dst": dst, "edge_attr": edge_attr_96, "edge_weight": edge_weight,
        "w_edge_t": np.asarray(L0_gnn_W_edge).T, "b_edge": np.asarray(L0_gnn_b_edge).reshape(1, -1),
        "eps": np.asarray(L0_gnn_eps).reshape(1, 1), "w1_t": np.asarray(L0_gnn_W1).T,
        "b1": np.asarray(L0_gnn_b1).reshape(-1, 1), "w2_t": np.asarray(L0_gnn_W2).T,
        "b2": np.asarray(L0_gnn_b2).reshape(1, -1),
    }
    nc = bacc.Bacc("TRN2", target_bir_lowering=False, num_devices=1)
    arrays, args = {}, []
    for name, a in laid_out.items():
        a = np.ascontiguousarray(a)
        arrays[f"in_{name}"] = a
        args.append(nc.dram_tensor(f"in_{name}", a.shape, mb.dt.from_np(a.dtype), kind="ExternalInput").ap())
    out = nc.dram_tensor("out_h", x.shape, mb.dt.float32, kind="ExternalOutput").ap()
    gnn_kernel(nc, *args, out)
    r = run_bass_kernel_spmd(nc, [arrays], core_ids=[0])
    return r.results[0]["out_h"]
```

```python
import concourse.bass as bass
from concourse import mybir
from contextlib import ExitStack


def gnn_kernel(nc, x, src, dst, edge_attr, edge_weight, w_edge_t, b_edge, eps, w1_t, b1, w2_t, b2, out):
    fp32 = mybir.dt.float32
    i32 = mybir.dt.int32
    ALU = mybir.AluOpType
    ACT = mybir.ActivationFunctionType
    ENG = mybir.EngineType

    N, D = x.shape
    assert N == src.shape[0]
    P = 128
    G = 5
    BLK = G * P
    NB = N // BLK
    TAIL = N - NB * BLK
    NT = NB * G + 1
    PAIRS = NB // 2
    assert NB % 2 == 0 and 0 < TAIL <= P and NB < P
    WIDTHS = (2, 3, 4)
    WIDE = WIDTHS[-1]
    ROWS = (NB + 1) * BLK
    SPARE = BLK
    DIV, SHIFT = -(-1024 // G), 10
    assert all(t * DIV >> SHIFT == t // G for t in range(NT))
    ENTRY = 8
    SPAN, FIT = G, G + 1
    LEAD = 2
    REACH = G * (LEAD + 1) - WIDE
    LN_EPS = 1e-5
    BANK = 512

    def short(i, s):
        return isinstance(i, int) and 2 * i + s == NB

    def by_block(a, i, s):
        if short(i, s):
            return a[NB * BLK:N, :]
        return a[0:NB * BLK, :].rearrange("(b p g) d -> b p (g d)", p=P, g=G)[2 * i + s, :, :]

    def by_tile(a, i, s):
        if short(i, s):
            return a[NB * BLK:N, :].rearrange("(g p) d -> p g d", g=1)
        return a[0:NB * BLK, :].rearrange("(b g p) d -> b p g d", p=P, g=G)[2 * i + s, :, :, :]

    def table_block(t, i, s):
        return t[0:ROWS, :].rearrange("(b p g) d -> b p (g d)", p=P, g=G)[2 * i + s, :, :]

    def as_row(a, i, s):
        if short(i, s):
            return a.rearrange("(o n) -> o n", o=1)[:, NB * BLK:N].to_broadcast([TAIL, TAIL])
        r = a[0:NB * BLK].rearrange("(b o n) -> b o n", o=1, n=BLK)[2 * i + s, :, :]
        return r.to_broadcast([P, BLK])

    col = lambda a: a.rearrange("(n o) -> n o", o=1)
    src_c, dst_c, w_c = col(src), col(dst), col(edge_weight)

    table = [nc.dram_tensor(f"table{k}", [ROWS + SPARE, D], fp32, kind="Internal").ap() for k in range(2)]
    local_dram = nc.dram_tensor("local_dram", [N], fp32, kind="Internal").ap()
    h_dram = nc.dram_tensor("h_dram", [N, D], fp32, kind="Internal").ap()
    plan_dram = nc.dram_tensor("plan_dram", [NB + 1, ENTRY], i32, kind="Internal").ap()

    ctx = ExitStack()
    with ctx:
        def sb(name, shape, dt=fp32):
            return ctx.enter_context(nc.sbuf_tensor(name, shape, dt))

        def pb(name, shape):
            return ctx.enter_context(nc.psum_tensor(name, shape, fp32))

        def sem(name):
            return ctx.enter_context(nc.semaphore(name))

        ident = sb("ident", [P, P])
        after = sb("after", [P, BLK], mybir.dt.bfloat16)
        number_i = sb("number_i", [P, G], i32)
        spare_row = sb("spare_row", [P, G])
        window_row = sb("window_row", [P, WIDE])
        count_up = sb("count_up", [P, WIDE * P])
        we = sb("we", [D + 1, D])
        w1 = sb("w1", [D, D])
        w2 = sb("w2", [D + 1, D])
        b1c = sb("b1c", [D, 1])
        eps1 = sb("eps1", [P, 1])
        lneps = sb("lneps", [P, 1])
        one = sb("one", [P, 1])
        zeros = sb("zeros", [P, G * D])
        plan = sb("plan", [P, (NB + 1) * ENTRY], i32)
        span_all = sb("span_all", [1, 1], i32)

        src_col = sb("src_col", [P, (NB + 1) * G])
        local_col = sb("local_col", [P, (NB + 1) * G])
        w_col = sb("w_col", [P, (NB + 1) * G])

        nodes = sb("nodes", [P, NT * D])
        WORK = 9632
        work = sb("work", [P, WORK])
        attr_t = [sb(f"attr_t{s}", [D + 1, BLK]) for s in range(2)]
        hid_t = attr_t
        h_t = sb("h_t", [D, BLK])

        key_col = sb("key_col", [P, 2, G], i32)
        get_col = sb("get_col", [P, 2, G], i32)
        wgt = sb("wgt", [P, 2, G])
        count = sb("count", [P, 2, G])
        off_spare = sb("off_spare", [P, 2, G])
        off_last = sb("off_last", [P, 2, G])
        put_col = sb("put_col", [P, 2, G], i32)
        stats = sb("stats", [P, 2, G * 6])
        mv = sb("mv", [P, 2, G * 2])
        std = sb("std", [P, 2, G])
        rstd = sb("rstd", [P, 2, G])
        shift = sb("shift", [P, 2, G])

        class Area:
            def __init__(self, tensor, at=0):
                self.tensor, self.at = tensor, at

            def take_one(self, width, dt):
                self.at += width
                return self.tensor[:, self.at - width:self.at].bitcast(dt)

            def take(self, width, dt=fp32):
                a = self.tensor[:, self.at:self.at + 2 * width]
                self.at += 2 * width
                if dt is not fp32:
                    a = a.bitcast(dt)
                return a.rearrange("p (s w) -> p s w", s=2)

        class Buffers:
            pass

        key_off = zeros[:, 0:(NB + 1) * G]

        def places(groups):
            found = {}
            for a, z in groups:
                for k in range(a, z):
                    for g in range(k, z):
                        found[k, g] = len(found) * P
            return found

        HOT = WORK - G * WIDE * P
        hot = [work[:, HOT + g * WIDE * P:HOT + (g + 1) * WIDE * P] for g in range(G)]
        hot1 = [count_up] + hot[1:]
        F = Buffers()
        F.groups = [(0, 3), (3, G)]
        F.tri = places(F.groups)
        a = Area(work)
        F.attr, F.got, F.pre, F.msg = (a.take(G * D) for _ in range(4))
        assert a.at <= HOT
        a = Area(work)
        F.xin, F.hin = a.take(G * D), a.take_one(G * D, fp32).unsqueeze(1).to_broadcast([P, 2, G * D])
        F.key_row, F.local_row = [a.take_one(BLK, i32)] * 2, a.take(BLK)
        F.same, F.msg1, F.sums = a.take(len(F.tri) * P), a.take(G * D), a.take(G * D)
        assert a.at <= HOT + WIDE * P
        a = Area(work)
        F.ain, F.bin, F.ab, F.res = (a.take(G * D) for _ in range(4))
        a = Area(nodes)
        M = Buffers()
        M.groups = [(0, G)]
        M.tri = places(M.groups)
        M.attr, M.got, M.pre, M.msg, M.sums = (a.take(G * D) for _ in range(5))
        M.msg1 = M.msg
        M.key_row, M.same = [a.take_one(BLK, i32), a.take_one(BLK, i32)], a.take(len(M.tri) * P)
        M.xin, M.ain, M.hin, M.y, M.res, M.fin = (a.take(G * D) for _ in range(6))
        assert a.at <= NT * D
        count_i = hot[0].bitcast(i32)
        tile_src = work[:, BLK:2 * BLK].bitcast(i32)
        tile_w = work[:, 2 * BLK:3 * BLK]
        tile_f = work[:, 3 * BLK:5 * BLK]
        tile_dst = work[:, 0:BLK].bitcast(i32)
        least = work[:, 3840:3840 + G]
        most = work[:, 3850:3850 + G]
        least_i = work[:, 3860:3860 + G].bitcast(i32)
        most_i = work[:, 3870:3870 + G].bitcast(i32)
        first_i = work[:, 3880:3880 + G].bitcast(i32)
        end_i = work[:, 3890:3890 + G].bitcast(i32)
        spans = work[:, 3900:3900 + G]
        furthest = work[:, 3930:3931]
        past = work[:, 3931:3932]
        misfit = work[:, 3932:3933]
        entry = work[:, 3910:3910 + ENTRY].bitcast(i32)

        wide = [pb(f"wide{s}", [P, 2 * BANK]) for s in range(2)]
        mid = [pb(f"mid{s}", [P, BANK]) for s in range(2)]
        tot_ps = [pb(f"tot_ps{s}", [P, BANK]) for s in range(2)]
        F.out_ps, F.sum_ps = [tot_ps[1]] * 2, [tot_ps[0]] * 2
        M.out_ps, M.sum_ps = mid, tot_ps
        F.back, M.back = 1, 2

        s_pool_go = sem("s_pool_go")
        s_sp_go = sem("s_sp_go")
        s_dve_go = sem("s_dve_go")
        s_wts = sem("s_wts")
        s_const = sem("s_const")
        s_iota = sem("s_iota")
        s_number = sem("s_number")
        s_eps = sem("s_eps")
        s_zero = sem("s_zero")
        s_cleared = sem("s_cleared")
        s_nodes0 = sem("s_nodes0")
        s_ones = sem("s_ones")
        s_dst = sem("s_dst")
        s_step = sem("s_step")
        s_rows = sem("s_rows")
        s_float = sem("s_float")
        s_turned = sem("s_turned")
        s_cols = sem("s_cols")
        s_get = sem("s_get")
        s_local = sem("s_local")
        s_first = sem("s_first")
        s_entry = sem("s_entry")
        s_plan_out = sem("s_plan_out")
        s_plan = sem("s_plan")
        s_span = sem("s_span")

        class Edge:
            def __init__(self, tag):
                two = lambda name: [sem(f"{tag}_{name}{s}") for s in range(2)]
                self.key_in, self.get_in, self.load_in = two("key_in"), two("get_in"), two("load_in")
                self.got_in = two("got_in")
                self.put_done = [two("put_even"), two("put_odd")]
                self.hot = sem(f"{tag}_hot")
                self.far = sem(f"{tag}_far")
                self.hot_act = sem(f"{tag}_hot_act")
                self.win_mm = sem(f"{tag}_win_mm")
                self.win_add = sem(f"{tag}_win_add")
                self.matched = sem(f"{tag}_matched")
                self.last = sem(f"{tag}_last")
                self.put_ready = sem(f"{tag}_put_ready")
                self.attr_tp = sem(f"{tag}_attr_tp")
                self.attr_ts = sem(f"{tag}_attr_ts")
                self.ea_mm = sem(f"{tag}_ea_mm")
                self.added = sem(f"{tag}_added")
                self.msg_ready = sem(f"{tag}_msg_ready")
                self.sum_mm = sem(f"{tag}_sum_mm")
                self.sums_ready = sem(f"{tag}_sums_ready")

        class Node:
            def __init__(self, tag):
                two = lambda name: [sem(f"{tag}_{name}{s}") for s in range(2)]
                self.x_in, self.stored = two("x_in"), two("stored")
                self.h = sem(f"{tag}_h")
                self.tp = sem(f"{tag}_tp")
                self.ts = sem(f"{tag}_ts")
                self.hid_mm = sem(f"{tag}_hid_mm")
                self.hid = sem(f"{tag}_hid")
                self.out_mm = sem(f"{tag}_out_mm")
                self.ab = sem(f"{tag}_ab")
                self.y = sem(f"{tag}_y")
                self.stats = sem(f"{tag}_stats")
                self.mv = sem(f"{tag}_mv")
                self.std = sem(f"{tag}_std")
                self.rstd = sem(f"{tag}_rstd")
                self.res = sem(f"{tag}_res")
                self.kept = two("kept")
                self.shift = sem(f"{tag}_shift")

        e0, e1 = Edge("e0"), Edge("e1")
        n0, n1 = Node("n0"), Node("n1")

        def had(i, s, back):
            return not isinstance(i, int) or 2 * i + s >= back

        def size(i, s):
            return (1, TAIL) if short(i, s) else (G, P)

        def steps(eng, *stages):
            lead = max(ahead for ahead, _ in stages)
            behind = max(0, -min(ahead for ahead, _ in stages))

            def step(i, s):
                for ahead, stage in stages:
                    o = s + ahead
                    if not isinstance(i, int) or 0 <= 2 * i + o <= NB:
                        stage(i + o // 2, o % 2)

            start = 1 + (behind + 1) // 2
            end = (NB - 2 - lead) // 2 + 1
            for n in range(-lead, 2 * start):
                step(n // 2, n % 2)
            with eng.Fori(start, end) as i:
                step(i, 0)
                step(i, 1)
            for n in range(2 * end, NB + 1 + behind):
                step(n // 2, n % 2)

        def put_before(eng, e, m, i, s):
            for q, (a, z) in enumerate(m.groups):
                eng.wait_ge(e.put_done[s][q], 16 * (z - a) * i)

        def put_all(eng, e, m):
            for s in range(2):
                for q, (a, z) in enumerate(m.groups):
                    eng.wait_ge(e.put_done[s][q], 16 * (z - a) * PAIRS + (16 if s == q == 0 else 0))

        def gathered(i, s):
            return 16 * G * i + 16 if short(i, s) else 16 * G * (i + 1)

        def entry_of(i, s, a, b):
            at = (2 * i + s) * ENTRY
            return plan[:, bass.ds(at + a, b - a)] if not isinstance(i, int) else plan[:, at + a:at + b]

        def edge_cols(a, i, s):
            at, n = (2 * i + s) * G, size(i, s)[0]
            return a[:, bass.ds(at, n)] if not isinstance(i, int) else a[:, at:at + n]

        def by_span(eng, span, by_width, widths=WIDTHS):
            if len(widths) == 1:
                by_width(widths[0])
                return
            with eng.If(span < widths[0]):
                by_width(widths[0])
            with eng.Else():
                by_span(eng, span, by_width, widths[1:])

        def own(i, s):
            at, width = (2 * i + s) * G * D, size(i, s)[0] * D
            return nodes[:, bass.ds(at, width)] if not isinstance(i, int) else nodes[:, at:at + width]

        def y_of(m, i, s):
            return own(i, s) if m is F else m.y[:, s, :]

        to_act, to_pool, to_dve = NT * 46 // 100 * D, NT * 69 // 100 * D, NT * 82 // 100 * D

        def window(first, w):
            return nodes[:, bass.ds(first * D, w * D)]

        CLEARS = 2 * (NB + 2)
        AHEAD = LEAD + 2

        block = ctx.enter_context(nc.Block())

        @block.sync
        def _(sp):
            reps = BLK // TAIL
            assert reps * TAIL == BLK
            for rows_1d, to, done in ((dst, tile_dst, s_dst), (src, tile_src, s_rows), (edge_weight, tile_w, s_rows)):
                sp.dma_start(to[0:NB, :], rows_1d[0:NB * BLK].rearrange("(b n) -> b n", n=BLK)).then_inc(done, 16)
                sp.dma_start(to[NB:NB + 1, :].rearrange("o (r n) -> o r n", r=reps),
                             rows_1d[NB * BLK:N].rearrange("(o r n) -> o r n", o=1, r=1)
                             .to_broadcast([1, reps, TAIL])).then_inc(done, 16)
            sp.dma_start(we[0:D, :], w_edge_t).then_inc(s_wts, 16)
            sp.dma_start(we[D:D + 1, :], b_edge).then_inc(s_wts, 16)
            sp.dma_start(w1[:, :], w1_t).then_inc(s_wts, 16)
            sp.dma_start(w2[0:D, :], w2_t).then_inc(s_wts, 16)
            sp.dma_start(w2[D:D + 1, :], b2).then_inc(s_wts, 16)
            sp.dma_start(b1c[:, :], b1).then_inc(s_wts, 16)
            sp.dma_start(eps1[:, :], eps.to_broadcast([P, 1])).then_inc(s_wts, 16)
            sp.wait_ge(s_entry, 2)
            sp.dma_start(plan_dram, entry[0:NB + 1, :]).then_inc(s_plan_out, 16)
            sp.wait_ge(s_plan_out, 16)
            sp.dma_start(plan[:, :], plan_dram.rearrange("(o b) e -> o (b e)", o=1)
                         .to_broadcast([P, (NB + 1) * ENTRY])).then_inc(s_plan, 16)

            def load_keys(e, m, key_1d, key, i, s):
                tiles, rows = size(i, s)
                sp.dma_start(key_col[0:rows, s, 0:tiles], by_block(key, i, s)).then_inc(e.key_in[s], 16)
                sp.dma_start(m.key_row[s][0:rows, 0:tiles * rows], as_row(key_1d, i, s)).then_inc(e.key_in[s], 16)

            def general_load0(i, s):
                tiles, rows = size(i, s)
                if had(i, s, 2):
                    done = 2 * i + s - 1
                    sp.wait_ge(e0.attr_tp, done)
                    sp.wait_ge(e0.put_ready, done)
                    sp.sem_inc(s_sp_go, 1)
                    sp.wait_ge(e0.got_in[s], 16 * G * i)
                sp.dma_start(get_col[0:rows, s, 0:tiles], by_block(src_c, i, s)).then_inc(e0.get_in[s], 16)
                load_keys(e0, M, dst, dst_c, i, s)
                sp.dma_start(M.attr[0:rows, s, 0:tiles * D], by_block(edge_attr, i, s)).then_inc(e0.load_in[s], 16)

            def general_load1(i, s):
                tiles, rows = size(i, s)
                if had(i, s, 2):
                    done = 2 * i + s - 1
                    sp.wait_ge(e1.msg_ready, done)
                    sp.wait_ge(e1.put_ready, done)
                    sp.sem_inc(s_sp_go, 1)
                    sp.wait_ge(e1.got_in[s], 16 * G * i)
                sp.dma_start(get_col[0:rows, s, 0:tiles], by_block(dst_c, i, s)).then_inc(e1.get_in[s], 16)
                load_keys(e1, M, src, src_c, i, s)
                sp.dma_start(wgt[0:rows, s, 0:tiles], by_block(w_c, i, s)).then_inc(e1.load_in[s], 16)

            def general_nodes(i, s):
                tiles, rows = size(i, s)
                if had(i, s, 2):
                    sp.wait_ge(n0.y, 2 * i + s - 1)
                sp.dma_start(M.xin[0:rows, s, 0:tiles * D], by_block(x, i, s)).then_inc(n0.x_in[s], 16)
                sp.dma_start(M.ain[0:rows, s, 0:tiles * D], by_block(table[0], i, s)).then_inc(n0.x_in[s], 16)

            def general_end(i, s):
                tiles, rows = size(i, s)
                if had(i, s, 2):
                    sp.wait_ge(n1.res, 2 * i + s - 1)
                sp.dma_start(M.fin[0:rows, s, 0:tiles * D], by_block(table[1], i, s)).then_inc(n1.x_in[s], 16)

            def fast_load0(i, s):
                tiles, rows = size(i, s)
                if had(i, s, 2):
                    sp.wait_ge(e0.attr_tp, 2 * i + s - 1)
                sp.dma_start(F.attr[0:rows, s, 0:tiles * D].rearrange("p (g d) -> p g d", g=tiles),
                             by_tile(edge_attr, i, s)).then_inc(e0.load_in[s], 16)

            def fast_nodes(i, s):
                tiles, rows = size(i, s)
                if had(i, s, 2):
                    sp.wait_ge(n0.kept[s], 16 * i)
                    sp.sem_inc(s_sp_go, 1)
                sp.dma_start(F.xin[0:rows, s, 0:tiles * D].rearrange("p (g d) -> p g d", g=tiles),
                             by_tile(x, i, s)).then_inc(n0.x_in[s], 16)

            def keep_x(i, s):
                tiles, rows = size(i, s)
                sp.wait_ge(n0.h, 2 * i + s + 1)
                sp.sem_inc(s_sp_go, 1)
                sp.dma_start(own(i, s)[0:rows, :], F.xin[0:rows, s, 0:tiles * D]).then_inc(n0.kept[s], 16)

            def fast_keys(i, s):
                tiles, rows = size(i, s)
                if had(i, s, 1):
                    sp.wait_ge(e1.matched, 2 * i + s)
                    sp.sem_inc(s_sp_go, 1)
                sp.dma_start(F.key_row[s][0:rows, 0:tiles * rows], as_row(src, i, s)).then_inc(e1.key_in[s], 16)

            def fast_local(i, s):
                tiles, rows = size(i, s)
                if had(i, s, 2):
                    sp.wait_ge(e1.hot, 10 * i + 5 * s - 5)
                    sp.sem_inc(s_sp_go, 1)
                elif s == 0:
                    sp.wait_ge(e0.win_add, NB * G + 1)
                r = as_row(local_dram, i, s)
                if short(i, s):
                    r = local_dram.rearrange("(o n) -> o n", o=1)[:, NB * BLK:N].to_broadcast([P, TAIL])
                sp.dma_start(F.local_row[:, s, 0:tiles * rows], r).then_inc(e1.load_in[s], 16)

            def fast_end(i, s):
                tiles, rows = size(i, s)
                if had(i, s, 2):
                    sp.wait_ge(n1.ab, 2 * i + s - 1)
                for k, buf in enumerate((F.ain, F.bin)):
                    sp.dma_start(buf[0:rows, s, 0:tiles * D],
                                 table_block(table[k], i, s)[0:rows, 0:tiles * D]).then_inc(n1.x_in[s], 16)

            sp.wait_ge(s_plan, 16)
            sp.wait_ge(s_span, 1)
            fits = sp.value_load(span_all[0:1, 0:1], min_val=0, max_val=NT)
            with sp.If(fits < WIDE):
                sp.wait_ge(s_float, 1)
                sp.dma_start(local_dram[0:NB * BLK].rearrange("(b n) -> b n", n=BLK),
                             tile_f[0:NB, 0:BLK]).then_inc(s_local, 16)
                sp.dma_start(local_dram[NB * BLK:N].rearrange("(o n) -> o n", o=1),
                             tile_f[NB:NB + 1, 0:TAIL]).then_inc(s_local, 16)
                sp.wait_ge(s_local, 32)
                sp.wait_ge(s_cols, 3)
                steps(sp, (0, fast_load0))
                sp.wait_ge(e0.attr_tp, NB + 1)
                steps(sp, (AHEAD + 2, keep_x), (AHEAD + 3, fast_nodes), (3, fast_local), (2, fast_keys))
                put_all(sp, e1, F)
                steps(sp, (0, fast_end))
            with sp.Else():
                sp.wait_ge(s_nodes0, 3)
                steps(sp, (0, general_load0))
                put_all(sp, e0, M)
                steps(sp, (0, general_nodes))
                sp.wait_ge(n0.res, NB + 1)
                steps(sp, (0, general_load1))
                put_all(sp, e1, M)
                steps(sp, (0, general_end))

        @block.gpsimd
        def _(pool):
            nc.gpsimd.memset(ident[:, :], 1.0).then_inc(s_const, 1)
            nc.gpsimd.memset(after[:, :], 1.0).then_inc(s_const, 1)
            nc.gpsimd.iota(number_i[:, :], pattern=[[P, G]], base=0, channel_multiplier=1).then_inc(s_iota, 1)
            nc.gpsimd.iota(count_i, pattern=[[1, WIDE * P]], base=0, channel_multiplier=0).then_inc(s_iota, 1)
            pool.wait_ge(s_const, 2)
            nc.gpsimd.affine_select(out=ident[:, :], in_=ident[:, :], compare_op=ALU.is_equal, fill=0.0,
                                    base=0, pattern=[[-1, P]], channel_multiplier=1).then_inc(s_const, 1)
            nc.gpsimd.affine_select(out=after[:, :], in_=after[:, :], compare_op=ALU.is_ge, fill=0.0,
                                    base=0, pattern=[[1, BLK]], channel_multiplier=-1).then_inc(s_const, 1)

            def gather(e, rows_of, to, i, s):
                tiles, rows = size(i, s)
                after_i, after_s = i + (s + 1) // 2, (s + 1) % 2
                if to is F.got:
                    pool.wait_ge(s_get, 2 * i + s + 1)
                else:
                    pool.wait_ge(e.get_in[s], 16 * (i + 1))
                if had(i, s, 2):
                    pool.wait_ge(e.added if e is e0 else e.msg_ready, 2 * i + s - 1)
                pool.sem_inc(s_pool_go, 1)
                for g in range(tiles):
                    nc.gpsimd.indirect_dma_start(
                        to[0:rows, s, g * D:(g + 1) * D], None, rows_of,
                        bass.IndirectOffsetOnAxis(ap=get_col[0:rows, s, g:g + 1], axis=0),
                    ).then_inc(e.got_in[s], 16)
                    if to is F.got and g == G // 2:
                        get_rows(after_i, after_s)

            def get_rows(i, s):
                tiles, rows = size(i, s)
                if had(i, s, 2):
                    pool.wait_ge(e0.got_in[s], 16 * G * i)
                nc.gpsimd.tensor_copy(get_col[0:rows, s, 0:tiles],
                                      edge_cols(src_col, i, s)[0:rows, :]).then_inc(s_get, 1)

            def scatter(e, m, into, i, s):
                tiles, rows = size(i, s)
                for q, (a, z) in enumerate(m.groups):
                    if a >= tiles:
                        continue
                    pool.wait_ge(s_cleared, 16 * CLEARS)
                    if had(i, s, 1):
                        pool.wait_ge(e.put_done[1 - s][q], 16 * (z - a) * (i + s))
                    pool.wait_ge(e.put_ready, 2 * i + s + 1)
                    pool.wait_ge(e.sums_ready, 2 * i + s + 1)
                    pool.sem_inc(s_pool_go, 1)
                    for g in range(a, min(z, tiles)):
                        nc.gpsimd.indirect_dma_start(
                            into[q], bass.IndirectOffsetOnAxis(ap=put_col[0:rows, s, g:g + 1], axis=0),
                            m.sums[0:rows, s, g * D:(g + 1) * D], None, compute_op=ALU.add,
                        ).then_inc(e.put_done[s][q], 16)

            def add_tables(i, s):
                tiles, rows = size(i, s)
                pool.wait_ge(n1.x_in[s], 32 * (i + 1))
                if had(i, s, 2):
                    pool.wait_ge(n1.y, 2 * i + s - 1)
                nc.gpsimd.tensor_tensor(F.ab[0:rows, s, 0:tiles * D], F.ain[0:rows, s, 0:tiles * D],
                                        F.bin[0:rows, s, 0:tiles * D], ALU.add).then_inc(n1.ab, 1)

            nc.gpsimd.memset(nodes[:, to_act:to_pool], 0.0).then_inc(s_nodes0, 1)
            pool.wait_ge(s_span, 1)
            fits = pool.value_load(span_all[0:1, 0:1], min_val=0, max_val=NT)
            with pool.If(fits < WIDE):
                pool.wait_ge(s_cols, 3)
                pool.wait_ge(s_local, 32)
                get_rows(0, 0)
                steps(pool, (0, lambda *b: gather(e0, x, F.got, *b)))
                steps(pool, (0, lambda *b: scatter(e1, F, table, *b)))
                steps(pool, (0, add_tables))
            with pool.Else():
                pool.wait_ge(s_nodes0, 3)
                steps(pool, (1, lambda *b: gather(e0, x, M.got, *b)), (0, lambda *b: scatter(e0, M, (table[0],), *b)))
                pool.wait_ge(n0.stored[1], 32 * PAIRS)
                pool.wait_ge(n0.stored[0], 32 * PAIRS + 32)
                steps(pool, (1, lambda *b: gather(e1, h_dram, M.got, *b)), (0, lambda *b: scatter(e1, M, (table[1],), *b)))

        @block.scalar
        def _(act):
            def clear(i, s):
                for t in table:
                    act.dma_start(table_block(t, i, s), zeros[:, :]).then_inc(s_cleared, 16)
                    if short(i, s):
                        act.dma_start(t[ROWS:ROWS + SPARE, :].rearrange("(p g) d -> p (g d)", g=G),
                                      zeros[:, :]).then_inc(s_cleared, 16)

            def attr_to_sbuf(i, s):
                tiles, rows = size(i, s)
                m = (tiles - 1) * P + rows
                act.wait_ge(e0.attr_tp, 2 * i + s + 1)
                if had(i, s, 2):
                    act.wait_ge(e0.ea_mm, 2 * i + s - 1)
                nc.scalar.copy(attr_t[s][0:D, 0:m], wide[s][0:D, 0:m]).then_inc(e0.attr_ts, 1)

            def sums_to_sbuf(e, m, i, s):
                tiles, rows = size(i, s)
                act.wait_ge(e.sum_mm, 2 * i + s + 1)
                if had(i, s, 2):
                    put_before(act, e, m, i, s)
                nc.scalar.copy(m.sums[0:rows, s, 0:tiles * D], m.sum_ps[s][0:rows, 0:tiles * D]).then_inc(e.sums_ready, 1)

            def messages0(m, i, s):
                tiles, rows = size(i, s)
                act.wait_ge(e0.added, 2 * i + s + 1)
                if had(i, s, 2):
                    if m is F:
                        act.wait_ge(e0.win_mm, 10 * i + 5 * s - 5)
                    else:
                        act.wait_ge(e0.sum_mm, 2 * i + s - 1)
                nc.scalar.activation(m.msg[0:rows, s, 0:tiles * D], m.pre[0:rows, s, 0:tiles * D],
                                     ACT.Relu).then_inc(e0.msg_ready, 1)

            def messages1(i, s):
                tiles, rows = size(i, s)
                act.wait_ge(e1.win_mm, 10 * i + 5 * s + tiles)
                if had(i, s, 2):
                    act.wait_ge(e1.sum_mm, 2 * i + s - 1)
                for g in range(tiles):
                    ins = nc.scalar.activation(F.msg1[0:rows, s, g * D:(g + 1) * D], mid[s][0:rows, g * D:(g + 1) * D],
                                               ACT.Copy, scale=edge_cols(w_col, i, s)[0:rows, g:g + 1])
                ins.then_inc(e1.msg_ready, 1)

            def mark_last(i, s):
                if short(i, s):
                    return
                g = G - 1
                if had(i, s, 1):
                    act.wait_ge(e0.win_mm, 10 * i + 5 * s)
                nc.scalar.activation(hot[g][:, :], count_up[:, :], ACT.Abs, scale=-1.0,
                                     bias=edge_cols(local_col, i, s)[:, g:g + 1]).then_inc(e0.far, 1)
                act.wait_ge(e0.far, 2 * i + s + 1)
                nc.scalar.activation(hot[g][:, :], hot[g][:, :], ACT.Relu, scale=-1.0,
                                     bias=one[:, 0:1]).then_inc(e0.hot_act, 1)

            def turned_to_sbuf(i, s):
                tiles, rows = size(i, s)
                m = (tiles - 1) * P + rows
                act.wait_ge(n0.tp, 2 * i + s + 1)
                if had(i, s, 1):
                    act.wait_ge(n0.hid_mm, 2 * i + s)
                nc.scalar.copy(h_t[:, 0:m], wide[0][0:D, 0:m]).then_inc(n0.ts, 1)

            def hidden_to_sbuf(i, s):
                tiles, rows = size(i, s)
                m = (tiles - 1) * P + rows
                act.wait_ge(n0.hid_mm, 2 * i + s + 1)
                if had(i, s, 2):
                    act.wait_ge(n0.out_mm, 2 * i + s - 1)
                nc.scalar.activation(hid_t[s][0:D, 0:m], wide[1][0:D, 0:m], ACT.Relu,
                                     bias=b1c[:, 0:1]).then_inc(n0.hid, 1)

            def root(n, i, s):
                tiles, rows = size(i, s)
                act.wait_ge(n.mv, 2 * i + s + 1)
                if had(i, s, 2):
                    act.wait_ge(n.rstd, 2 * i + s - 1)
                nc.scalar.activation(std[0:rows, s, 0:tiles],
                                     mv[0:rows, s, 0:2 * tiles].rearrange("p (g k) -> p g k", k=2)[:, :, 1],
                                     ACT.Sqrt, bias=lneps[0:rows, 0:1]).then_inc(n.std, 1)

            def normalize(n, y, to, i, s):
                tiles, rows = size(i, s)
                act.wait_ge(n.shift, 2 * i + s + 1)
                for g in range(tiles):
                    ins = nc.scalar.activation(to[0:rows, g * D:(g + 1) * D], y[0:rows, g * D:(g + 1) * D],
                                               ACT.Identity, scale=rstd[0:rows, s, g:g + 1],
                                               bias=shift[0:rows, s, g:g + 1])
                ins.then_inc(n.res, 1)

            def end(m, i, s):
                if had(i, s, 2):
                    act.wait_ge(n1.stored[s], 16 * i)
                normalize(n1, own(i, s) if m is F else m.fin[:, s, :], m.res[:, s, :], i, s)

            def end0(i, s):
                if had(i, s, 2):
                    act.wait_ge(n0.stored[s], 32 * i)
                normalize(n0, M.y[:, s, :], M.res[:, s, :], i, s)
                store(n0, M.res, (h_dram, table[1][0:N, :]), False, i, s)

            def store(n, res, tables, tiled, i, s):
                tiles, rows = size(i, s)
                act.wait_ge(n.res, 2 * i + s + 1)
                for t in tables:
                    if tiled:
                        act.dma_start(by_tile(t, i, s), res[0:rows, s, 0:tiles * D]
                                      .rearrange("p (g d) -> p g d", g=tiles)).then_inc(n.stored[s], 16)
                    else:
                        act.dma_start(by_block(t, i, s), res[0:rows, s, 0:tiles * D]).then_inc(n.stored[s], 16)

            act.wait_ge(s_eps, 2)
            act.wait_ge(s_zero, 1)
            nc.scalar.activation(nodes[:, 0:to_act].rearrange("p (r w) -> p r w", w=D),
                                 zeros[:, 0:D].unsqueeze(1).to_broadcast([P, to_act // D, D]),
                                 ACT.Copy).then_inc(s_nodes0, 1)
            act.wait_ge(s_span, 1)
            fits = act.value_load(span_all[0:1, 0:1], min_val=0, max_val=NT)
            with act.If(fits < WIDE):
                steps(act, (3, attr_to_sbuf), (1, lambda *b: messages0(F, *b)), (0, mark_last), (3, clear))
                steps(act, (0, messages1), (AHEAD + 1, hidden_to_sbuf),
                      (AHEAD - 1, lambda *b: normalize(n0, own(*b), own(*b), *b)),
                      (-1, lambda *b: sums_to_sbuf(e1, F, *b)), (AHEAD + 2, turned_to_sbuf),
                      (AHEAD, lambda *b: root(n0, *b)))
                steps(act, (1, lambda *b: root(n1, *b)), (-1, lambda *b: store(n1, F.res, (out,), True, *b)),
                      (0, lambda *b: end(F, *b)))
            with act.Else():
                act.wait_ge(s_nodes0, 3)
                steps(act, (0, clear))
                steps(act, (1, attr_to_sbuf), (0, lambda *b: messages0(M, *b)), (0, lambda *b: sums_to_sbuf(e0, M, *b)))
                steps(act, (1, turned_to_sbuf), (1, hidden_to_sbuf), (0, lambda *b: root(n0, *b)), (-1, end0))
                steps(act, (0, lambda *b: sums_to_sbuf(e1, M, *b)))
                steps(act, (1, lambda *b: root(n1, *b)), (-1, lambda *b: store(n1, M.res, (out,), False, *b)),
                      (0, lambda *b: end(M, *b)))
            act.wait_ge(n1.stored[1], 16 * PAIRS)
            act.wait_ge(n1.stored[0], 16 * PAIRS + 16)

        @block.vector
        def _(dve):
            nc.vector.memset(zeros[:, :], 0.0).then_inc(s_zero, 1)
            nc.vector.memset(attr_t[0][D:D + 1, :], 1.0).then_inc(s_ones, 1)
            nc.vector.memset(attr_t[1][D:D + 1, :], 1.0).then_inc(s_ones, 1)
            nc.vector.memset(lneps[:, :], LN_EPS).then_inc(s_eps, 1)
            nc.vector.memset(one[:, :], 1.0).then_inc(s_eps, 1)
            nc.vector.memset(entry[0:NB + 1, :], 0).then_inc(s_step, 1)

            dve.wait_ge(s_dst, 32)
            cut = tile_dst[0:NB + 1, :].rearrange("b (g n) -> b g n", g=G)
            nc.vector.tensor_reduce(out=least[0:NB + 1, :], in_=cut, axis=mybir.AxisListType.X, op=ALU.min).then_inc(s_step, 1)
            nc.vector.tensor_reduce(out=most[0:NB + 1, :], in_=cut, axis=mybir.AxisListType.X, op=ALU.max).then_inc(s_step, 1)
            dve.wait_ge(s_step, 3)
            nc.vector.tensor_copy(least_i[0:NB + 1, :], least[0:NB + 1, :]).then_inc(s_step, 1)
            nc.vector.tensor_copy(most_i[0:NB + 1, :], most[0:NB + 1, :]).then_inc(s_step, 1)
            dve.wait_ge(s_step, 5)
            nc.vector.tensor_scalar(first_i[0:NB + 1, :], least_i[0:NB + 1, :], 7, None, ALU.arith_shift_right).then_inc(s_step, 1)
            nc.vector.tensor_scalar(end_i[0:NB + 1, :], most_i[0:NB + 1, :], 7, None, ALU.arith_shift_right).then_inc(s_step, 1)
            dve.wait_ge(s_step, 7)
            nc.vector.tensor_scalar(entry[0:NB + 1, 0:G], first_i[0:NB + 1, :], NT - WIDE, None, ALU.min).then_inc(s_step, 1)
            dve.wait_ge(s_step, 8)
            nc.vector.tensor_tensor(spans[0:NB + 1, :], end_i[0:NB + 1, :], entry[0:NB + 1, 0:G], ALU.subtract).then_inc(s_step, 1)
            dve.wait_ge(s_step, 9)
            nc.vector.tensor_reduce(out=entry[0:NB + 1, SPAN:SPAN + 1], in_=spans[0:NB + 1, :],
                                    axis=mybir.AxisListType.X, op=ALU.max).then_inc(s_entry, 1)
            nc.vector.tensor_reduce(out=furthest[0:NB + 1, :], in_=entry[0:NB + 1, 0:G],
                                    axis=mybir.AxisListType.X, op=ALU.max).then_inc(s_step, 1)
            dve.wait_ge(s_step, 10)
            dve.wait_ge(s_iota, 2)
            nc.vector.scalar_tensor_tensor(out=past[0:NB + 1, :], in0=number_i[0:NB + 1, 0:1], scalar=-float(G),
                                           in1=furthest[0:NB + 1, :], op0=ALU.mult, op1=ALU.add).then_inc(s_step, 1)
            dve.wait_ge(s_step, 11)
            nc.vector.tensor_scalar(misfit[0:NB + 1, :], past[0:NB + 1, :], float(REACH), float(WIDE),
                                    ALU.is_gt, ALU.mult).then_inc(s_step, 1)
            dve.wait_ge(s_step, 12)
            dve.wait_ge(s_entry, 1)
            nc.vector.tensor_tensor(entry[0:NB + 1, FIT:FIT + 1], entry[0:NB + 1, SPAN:SPAN + 1], misfit[0:NB + 1, :],
                                    ALU.max).then_inc(s_entry, 1)

            nc.vector.tensor_copy(window_row[:, :], number_i[:, 0:WIDE]).then_inc(s_number, 1)
            nc.vector.tensor_scalar(spare_row[:, :], number_i[:, 0:G], float(ROWS), None, ALU.add).then_inc(s_number, 1)
            nc.vector.tensor_copy(count_up[:, :], count_i).then_inc(s_number, 1)
            dve.wait_ge(s_wts, 16 * 7)
            nc.vector.tensor_scalar(eps1[:, :], eps1[:, :], 1.0, None, ALU.add).then_inc(s_number, 1)
            nc.vector.memset(nodes[:, to_pool:to_dve], 0.0).then_inc(s_nodes0, 1)
            dve.wait_ge(s_number, 4)
            dve.wait_ge(s_const, 4)
            dve.wait_ge(s_plan, 16)
            nc.vector.tensor_reduce(out=span_all[0:1, 0:1],
                                    in_=plan[0:1, :].rearrange("o (b e) -> o b e", e=ENTRY)[:, :, FIT],
                                    axis=mybir.AxisListType.X, op=ALU.max).then_inc(s_span, 1)

            def match(e, m, tiled, i, s):
                tiles, rows = size(i, s)
                dve.wait_ge(e.key_in[s], (16 if tiled else 32) * (i + 1))
                if had(i, s, 2):
                    dve.wait_ge(e.sum_mm, 2 * i + s - 1)
                own_key = edge_cols(src_col, i, s) if tiled else key_col[:, s, 0:tiles]
                keys = m.key_row[s][0:rows, 0:tiles * rows]
                by_g = keys.rearrange("k (g p) -> k g p" if tiled else "k (p g) -> k g p", g=tiles)
                for g in range(tiles):
                    end_ = min(tiles, next(z for a, z in m.groups if a <= g < z))
                    n = end_ - g
                    out_ = m.same[0:rows, s, m.tri[g, g]:m.tri[g, g] + (n - 1) * P + rows]
                    ins = nc.vector.scalar_tensor_tensor(
                        out=out_.rearrange("k (g p) -> k g p", g=n),
                        in0=by_g[:, g:end_, :], scalar=own_key[0:rows, g:g + 1],
                        in1=after[0:rows, 0:(n - 1) * P + rows].rearrange("k (g p) -> k g p", g=n),
                        op0=ALU.is_equal, op1=ALU.mult, accum_out=count[0:rows, s, g:g + 1])
                ins.then_inc(e.matched, 1)

            def pick_last(e, tiled, i, s):
                tiles, rows = size(i, s)
                own_key = edge_cols(src_col, i, s) if tiled else key_col[:, s, 0:tiles]
                off = edge_cols(key_off, i, s)[0:rows, :]
                if not tiled:
                    off = off_spare[0:rows, s, 0:tiles]
                    nc.vector.tensor_tensor(off, own_key[0:rows, :], spare_row[0:rows, 0:tiles],
                                            ALU.subtract).then_inc(s_first, 1)
                    dve.wait_ge(s_first, 2 * i + s + (1 if e is e0 else NB + 2))
                dve.wait_ge(e.matched, 2 * i + s + 1)
                nc.vector.scalar_tensor_tensor(
                    out=off_last[0:rows, s, 0:tiles], in0=count[0:rows, s, 0:tiles], scalar=1.0, in1=off,
                    op0=ALU.is_equal, op1=ALU.mult).then_inc(e.last, 1)

            def aim(e, m, i, s):
                tiles, rows = size(i, s)
                dve.wait_ge(e.last, 2 * i + s + 1)
                if had(i, s, 2):
                    put_before(dve, e, m, i, s)
                nc.vector.tensor_tensor(put_col[0:rows, s, 0:tiles], off_last[0:rows, s, 0:tiles],
                                        spare_row[0:rows, 0:tiles], ALU.add).then_inc(e.put_ready, 1)

            def add_x(m, i, s):
                tiles, rows = size(i, s)
                dve.wait_ge(e0.ea_mm, 2 * i + s + 1)
                dve.wait_ge(e0.got_in[s], gathered(i, s))
                if had(i, s, 2):
                    dve.wait_ge(e0.msg_ready, 2 * i + s - 1)
                nc.vector.tensor_tensor(m.pre[0:rows, s, 0:tiles * D], mid[s][0:rows, 0:tiles * D],
                                        m.got[0:rows, s, 0:tiles * D], ALU.add).then_inc(e0.added, 1)

            def to_columns():
                dve.wait_ge(s_rows, 64)
                cut = lambda a: a.rearrange("b (g n) -> b g n", g=G)
                nc.vector.scalar_tensor_tensor(
                    out=cut(tile_f[0:NB + 1, 0:BLK]), in0=entry[0:NB + 1, 0:G].unsqueeze(2).to_broadcast([NB + 1, G, P]),
                    scalar=-float(P), in1=cut(tile_dst[0:NB + 1, :]), op0=ALU.mult, op1=ALU.add).then_inc(s_float, 1)
                nc.vector.tensor_copy(tile_f[0:NB + 1, BLK:2 * BLK], tile_src[0:NB + 1, :]).then_inc(s_float, 1)
                for k, to in enumerate((local_col, src_col, w_col)):
                    dve.wait_ge(s_turned, k + 1)
                    nc.vector.tensor_copy(to[:, :].rearrange("p (b g) -> p g b", g=G),
                                          wide[k % 2][:, 0:G * P].rearrange("p (g b) -> p g b", g=G)[:, :, 0:NB + 1]
                                          ).then_inc(s_cols, 1)
                dve.wait_ge(s_cols, 3)
                dve.wait_ge(s_local, 32)

            def windows_of(i, s):
                at = entry_of(i, s, 0, ENTRY)
                _, v = nc.values_load_multi_w_load_instructions(
                    at[0:1, 0:SPAN + 1], engines=(ENG.DVE,), min_val=0, max_val=NT - WIDE,
                    skip_runtime_bounds_check_because="the plan holds windows inside the nodes")
                return v[0:G], v[SPAN]

            def mark(i, s, g):
                rows = size(i, s)[1]
                if had(i, s, 1):
                    dve.wait_ge(e0.win_mm, 10 * i + 5 * s + g - 4)
                nc.vector.tensor_scalar(hot[g][0:rows, :], count_up[0:rows, :], edge_cols(local_col, i, s)[0:rows, g:g + 1], None,
                                        ALU.is_equal).then_inc(e0.hot, 1)

            def window_sums(i, s):
                tiles, rows = size(i, s)
                after_i, after_s = i + (s + 1) // 2, (s + 1) % 2
                ahead = 0 if short(i, s) else size(after_i, after_s)[0]
                first, span = windows_of(i, s)

                def by_width(w):
                    for g in range(tiles):
                        t = 10 * i + 5 * s + g
                        dve.wait_ge(e0.win_mm, t + 1)
                        if had(i, s, 1) or g >= 1:
                            dve.wait_ge(e0.win_add, t)
                        nc.vector.tensor_tensor(window(first[g], w), window(first[g], w),
                                                tot_ps[(s + g) % 2][:, 0:w * D], ALU.add).then_inc(e0.win_add, 1)
                        if g < min(ahead, G - 1):
                            mark(after_i, after_s, g)

                by_span(dve, span, by_width)

            def layer1_columns(i, s):
                if not isinstance(i, int) or (i, s) != (0, 0):
                    return
                dve.wait_ge(s_cleared, 16 * CLEARS)
                width = (NB + 1) * G
                node = local_col[:, :].bitcast(i32)
                tile_ = count_up[:, 0:width].bitcast(i32)
                block_ = key_off.bitcast(i32)
                nc.vector.tensor_copy(node, src_col[:, :]).then_inc(s_first, 1)
                dve.wait_ge(s_first, 1)
                nc.vector.tensor_scalar(tile_, node, P.bit_length() - 1, None, ALU.arith_shift_right).then_inc(s_first, 1)
                dve.wait_ge(s_first, 2)
                nc.vector.tensor_scalar(node, node, P - 1, None, ALU.bitwise_and).then_inc(s_first, 1)
                nc.vector.tensor_scalar(block_, tile_, float(DIV), None, ALU.mult).then_inc(s_first, 1)
                dve.wait_ge(s_first, 4)
                nc.vector.tensor_scalar(block_, block_, SHIFT, None, ALU.arith_shift_right).then_inc(s_first, 1)
                nc.vector.scalar_tensor_tensor(out=tile_, in0=node, scalar=float(G), in1=tile_,
                                               op0=ALU.mult, op1=ALU.add).then_inc(s_first, 1)
                dve.wait_ge(s_first, 6)
                nc.vector.scalar_tensor_tensor(out=key_off, in0=block_, scalar=float(BLK - G), in1=tile_,
                                               op0=ALU.mult, op1=ALU.add).then_inc(s_first, 1)
                dve.wait_ge(s_first, 7)
                by_block_ = key_off.rearrange("p (b g) -> p b g", g=G)
                nc.vector.tensor_tensor(by_block_, by_block_, spare_row[:, :].unsqueeze(1).to_broadcast([P, NB + 1, G]),
                                        ALU.subtract).then_inc(s_first, 1)
                dve.wait_ge(s_first, 8)

            def form_h(m, i, s):
                tiles, rows = size(i, s)
                dve.wait_ge(n0.x_in[s], (32 if m is M else 16) * (i + 1))
                if had(i, s, m.back):
                    dve.wait_ge(n0.tp, 2 * i + s + 1 - m.back)
                sums = m.ain[0:rows, s, 0:tiles * D] if m is M else own(i, s)[0:rows, :]
                nc.vector.scalar_tensor_tensor(
                    out=m.hin[0:rows, s, 0:tiles * D], in0=m.xin[0:rows, s, 0:tiles * D], scalar=eps1[0:rows, 0:1],
                    in1=sums, op0=ALU.mult, op1=ALU.add).then_inc(n0.h, 1)

            def residual(m, i, s):
                tiles, rows = size(i, s)
                dve.wait_ge(n0.out_mm, 2 * i + s + 1)
                if m is F:
                    dve.wait_ge(n0.kept[s], 16 * (i + 1))
                elif had(i, s, 2):
                    dve.wait_ge(n0.res, 2 * i + s - 1)
                x_in = own(i, s)[0:rows, :] if m is F else m.xin[0:rows, s, 0:tiles * D]
                nc.vector.tensor_tensor(y_of(m, i, s)[0:rows, 0:tiles * D], m.out_ps[s][0:rows, 0:tiles * D],
                                        x_in, ALU.add).then_inc(n0.y, 1)

            def statistics(n, y, i, s):
                tiles, rows = size(i, s)
                for g in range(tiles):
                    ins = nc.vector.bn_stats(out=stats[0:rows, s, 6 * g:6 * g + 6], in_=y[0:rows, g * D:(g + 1) * D])
                ins.then_inc(n.stats, 1)

            def mean_and_variance(n, i, s):
                tiles, rows = size(i, s)
                dve.wait_ge(n.stats, 2 * i + s + 1)
                if had(i, s, 2):
                    dve.wait_ge(n.shift, 2 * i + s - 1)
                dve.sem_inc(s_dve_go, 1)
                for g in range(tiles):
                    ins = nc.vector.bn_aggr(out=mv[0:rows, s, 2 * g:2 * g + 2], in_=stats[0:rows, s, 6 * g:6 * g + 6])
                ins.then_inc(n.mv, 1)

            def invert_root(n, i, s):
                tiles, rows = size(i, s)
                dve.wait_ge(n.std, 2 * i + s + 1)
                if had(i, s, 2):
                    dve.wait_ge(n.res, 2 * i + s - 1)
                nc.vector.reciprocal(rstd[0:rows, s, 0:tiles], std[0:rows, s, 0:tiles]).then_inc(n.rstd, 1)

            def shifts(n, i, s):
                tiles, rows = size(i, s)
                dve.wait_ge(n.rstd, 2 * i + s + 1)
                nc.vector.scalar_tensor_tensor(
                    out=shift[0:rows, s, 0:tiles], in0=mv[0:rows, s, 0:2 * tiles].rearrange("p (g k) -> p g k", k=2)[:, :, 0],
                    scalar=-1.0, in1=rstd[0:rows, s, 0:tiles], op0=ALU.mult, op1=ALU.mult).then_inc(n.shift, 1)

            def statistics0(m, i, s):
                dve.wait_ge(n0.y, 2 * i + s + 1)
                dve.sem_inc(s_dve_go, 1)
                statistics(n0, y_of(m, i, s), i, s)

            def weigh(i, s):
                tiles, rows = size(i, s)
                dve.wait_ge(e1.load_in[s], 16 * (i + 1))
                dve.wait_ge(e1.got_in[s], gathered(i, s))
                if had(i, s, 2):
                    dve.wait_ge(e1.sum_mm, 2 * i + s - 1)
                cut3 = lambda a: a[0:rows, s, 0:tiles * D].rearrange("p (g d) -> p g d", g=tiles)
                nc.vector.tensor_tensor(cut3(M.msg), cut3(M.got),
                                        wgt[0:rows, s, 0:tiles].unsqueeze(2).to_broadcast([rows, tiles, D]),
                                        ALU.mult).then_inc(e1.msg_ready, 1)

            def window_marks(i, s):
                tiles, rows = size(i, s)
                _, (span,) = nc.values_load_multi_w_load_instructions(
                    entry_of(i, s, SPAN, SPAN + 1)[0:1, :], engines=(ENG.DVE,), min_val=0, max_val=NT,
                    skip_runtime_bounds_check_because="it only picks the window's width")
                dve.wait_ge(e1.load_in[s], 16 * (i + 1))
                dve.sem_inc(s_dve_go, 1)

                def by_width(w):
                    for g in range(tiles):
                        if had(i, s, 1):
                            dve.wait_ge(e1.win_mm, 10 * i + 5 * s + g - 4)
                        nc.vector.tensor_tensor(
                            hot1[g][:, 0:w * P].rearrange("p (j e) -> p j e", j=w)[:, :, 0:rows],
                            F.local_row[:, s, g * P:g * P + rows].unsqueeze(1).to_broadcast([P, w, rows]),
                            window_row[:, 0:w].unsqueeze(2).to_broadcast([P, w, rows]),
                            ALU.is_equal).then_inc(e1.hot, 1)

                by_span(dve, span, by_width)

            def add_h(i, s):
                tiles, rows = size(i, s)
                dve.wait_ge(n1.ab, 2 * i + s + 1)
                nc.vector.tensor_tensor(own(i, s)[0:rows, :], F.ab[0:rows, s, 0:tiles * D],
                                        own(i, s)[0:rows, :], ALU.add).then_inc(n1.y, 1)

            def statistics1(i, s):
                dve.wait_ge(n1.y, 2 * i + s + 1)
                dve.sem_inc(s_dve_go, 1)
                statistics(n1, own(i, s), i, s)

            def general_statistics(i, s):
                dve.wait_ge(n1.x_in[s], 16 * (i + 1))
                statistics(n1, M.fin[:, s, :], i, s)

            dve.wait_ge(s_rows, 64)
            dve.wait_ge(s_span, 1)
            fits = dve.value_load(span_all[0:1, 0:1], min_val=0, max_val=NT)
            with dve.If(fits < WIDE):
                to_columns()
                nc.vector.memset(nodes[:, to_dve:NT * D], 0.0).then_inc(s_nodes0, 1)
                dve.wait_ge(s_nodes0, 4)
                for g in range(G - 1):
                    mark(0, 0, g)
                steps(dve, (1, lambda *b: add_x(F, *b)), (0, window_sums))
                dve.wait_ge(e0.win_add, NB * G + 1)
                steps(dve, (AHEAD, lambda *b: residual(F, *b)), (AHEAD + 2, lambda *b: form_h(F, *b)),
                      (AHEAD + 1, layer1_columns), (AHEAD - 1, lambda *b: shifts(n0, *b)), (0, lambda *b: pick_last(e1, True, *b)),
                      (AHEAD, lambda *b: statistics0(F, *b)), (1, window_marks),
                      (AHEAD, lambda *b: mean_and_variance(n0, *b)), (1, lambda *b: match(e1, F, True, *b)),
                      (0, lambda *b: aim(e1, F, *b)), (AHEAD, lambda *b: invert_root(n0, *b)))
                steps(dve, (1, add_h), (0, lambda *b: invert_root(n1, *b)), (1, statistics1),
                      (0, lambda *b: shifts(n1, *b)), (1, lambda *b: mean_and_variance(n1, *b)))
            with dve.Else():
                dve.wait_ge(s_nodes0, 3)
                steps(dve, (1, lambda *b: match(e0, M, False, *b)), (0, lambda *b: pick_last(e0, False, *b)),
                      (0, lambda *b: add_x(M, *b)), (0, lambda *b: aim(e0, M, *b)))
                steps(dve, (1, lambda *b: form_h(M, *b)), (0, lambda *b: residual(M, *b)),
                      (0, lambda *b: statistics0(M, *b)), (0, lambda *b: mean_and_variance(n0, *b)),
                      (-1, lambda *b: invert_root(n0, *b)), (-1, lambda *b: shifts(n0, *b)))
                steps(dve, (1, lambda *b: match(e1, M, False, *b)), (0, weigh),
                      (0, lambda *b: pick_last(e1, False, *b)), (0, lambda *b: aim(e1, M, *b)))
                steps(dve, (1, general_statistics), (1, lambda *b: mean_and_variance(n1, *b)),
                      (0, lambda *b: invert_root(n1, *b)), (0, lambda *b: shifts(n1, *b)))

        @block.tensor
        def _(pe):
            pe.wait_ge(s_const, 4)
            pe.wait_ge(s_wts, 16 * 7)
            pe.wait_ge(s_ones, 2)

            def turn_attr(m, i, s):
                tiles, rows = size(i, s)
                pe.wait_ge(e0.load_in[s], 16 * (i + 1))
                if had(i, s, 2):
                    pe.wait_ge(e0.attr_ts, 2 * i + s - 1)
                for g in range(tiles):
                    ins = nc.tensor.transpose(wide[s][0:D, g * P:g * P + rows], m.attr[0:rows, s, g * D:(g + 1) * D],
                                              ident[0:rows, 0:rows])
                ins.then_inc(e0.attr_tp, 1)

            def edge_linear(i, s):
                tiles, rows = size(i, s)
                pe.wait_ge(e0.attr_ts, 2 * i + s + 1)
                if had(i, s, 2):
                    pe.wait_ge(e0.added, 2 * i + s - 1)
                for g in range(tiles):
                    ins = nc.tensor.matmul(mid[s][0:rows, g * D:(g + 1) * D], attr_t[s][:, g * P:g * P + rows],
                                           we[:, :], start=True, stop=True)
                ins.then_inc(e0.ea_mm, 1)

            def window_products(i, s):
                tiles, rows = size(i, s)
                _, (span,) = nc.values_load_multi_w_load_instructions(
                    entry_of(i, s, SPAN, SPAN + 1)[0:1, :], engines=(ENG.PE,), min_val=0, max_val=NT,
                    skip_runtime_bounds_check_because="it only picks the window's width")
                pe.wait_ge(e0.msg_ready, 2 * i + s + 1)

                def by_width(w):
                    for g in range(tiles):
                        t = 10 * i + 5 * s + g
                        if g < G - 1:
                            pe.wait_ge(e0.hot, 8 * i + 4 * s + g + 1)
                        else:
                            pe.wait_ge(e0.hot_act, 2 * i + s + 1)
                        if had(i, s, 1) or g >= 2:
                            pe.wait_ge(e0.win_add, t - 1)
                        k = (s + g) % 2
                        for j in range(w):
                            ins = nc.tensor.matmul(tot_ps[k][:, j * D:(j + 1) * D], hot[g][0:rows, j * P:(j + 1) * P],
                                                   F.msg[0:rows, s, g * D:(g + 1) * D], start=True, stop=True)
                        ins.then_inc(e0.win_mm, 1)

                by_span(pe, span, by_width)

            def window_gather(i, s):
                tiles, rows = size(i, s)
                _, v = nc.values_load_multi_w_load_instructions(
                    entry_of(i, s, 0, SPAN + 1)[0:1, :], engines=(ENG.PE,), min_val=0, max_val=NT - WIDE,
                    skip_runtime_bounds_check_because="the plan holds windows inside the nodes")
                first, span = v[0:G], v[SPAN]
                done = 2 * i + s + LEAD + 1
                pe.wait_ge(n0.res, min(done, NB + 1) if isinstance(i, int) else done)
                if had(i, s, 2):
                    pe.wait_ge(e1.msg_ready, 2 * i + s - 1)

                def by_width(w):
                    for g in range(tiles):
                        pe.wait_ge(e1.hot, 10 * i + 5 * s + g + 1)
                        for j in range(w):
                            ins = nc.tensor.matmul(mid[s][0:rows, g * D:(g + 1) * D], hot1[g][:, j * P:j * P + rows],
                                                   nodes[:, bass.ds(first[g] * D + j * D, D)],
                                                   start=(j == 0), stop=(j == w - 1))
                        ins.then_inc(e1.win_mm, 1)

                by_span(pe, span, by_width)

            def block_sums(e, m, i, s):
                tiles, rows = size(i, s)
                pe.wait_ge(e.matched, 2 * i + s + 1)
                pe.wait_ge(e.msg_ready, 2 * i + s + 1)
                if had(i, s, m.back):
                    pe.wait_ge(e.sums_ready, 2 * i + s + 1 - m.back)
                for g in range(tiles):
                    first = next(a for a, z in m.groups if a <= g < z)
                    for k in range(first, g + 1):
                        ins = nc.tensor.matmul(m.sum_ps[s][0:rows, g * D:(g + 1) * D],
                                               m.same[0:rows, s, m.tri[k, g]:m.tri[k, g] + rows],
                                               m.msg1[0:rows, s, k * D:(k + 1) * D], start=(k == first), stop=(k == g))
                ins.then_inc(e.sum_mm, 1)

            def turn_h(m, i, s):
                tiles, rows = size(i, s)
                pe.wait_ge(n0.h, 2 * i + s + 1)
                if had(i, s, 1):
                    pe.wait_ge(n0.ts, 2 * i + s)
                for g in range(tiles):
                    ins = nc.tensor.transpose(wide[0][0:D, g * P:g * P + rows], m.hin[0:rows, s, g * D:(g + 1) * D],
                                              ident[0:rows, 0:rows])
                ins.then_inc(n0.tp, 1)

            def hidden(i, s):
                tiles, rows = size(i, s)
                n = (tiles - 1) * P + rows
                pe.wait_ge(n0.ts, 2 * i + s + 1)
                if had(i, s, 1):
                    pe.wait_ge(n0.hid, 2 * i + s)
                for at in range(0, n, BANK):
                    to = min(n, at + BANK)
                    ins = nc.tensor.matmul(wide[1][0:D, at:to], w1[:, :], h_t[:, at:to], start=True, stop=True)
                ins.then_inc(n0.hid_mm, 1)

            def project(m, i, s):
                tiles, rows = size(i, s)
                pe.wait_ge(n0.hid, 2 * i + s + 1)
                if had(i, s, m.back):
                    pe.wait_ge(n0.y, 2 * i + s + 1 - m.back)
                for g in range(tiles):
                    ins = nc.tensor.matmul(m.out_ps[s][0:rows, g * D:(g + 1) * D], hid_t[s][:, g * P:g * P + rows],
                                           w2[:, :], start=True, stop=True)
                ins.then_inc(n0.out_mm, 1)

            pe.wait_ge(s_plan, 16)
            pe.wait_ge(s_span, 1)
            fits = pe.value_load(span_all[0:1, 0:1], min_val=0, max_val=NT)
            with pe.If(fits < WIDE):
                pe.wait_ge(s_float, 2)
                pe.wait_ge(s_rows, 64)
                for k, rows_f in enumerate((tile_f[:, 0:BLK], tile_f[:, BLK:2 * BLK], tile_w)):
                    if k == 2:
                        pe.wait_ge(s_cols, 1)
                    for g in range(G):
                        ins = nc.tensor.transpose(wide[k % 2][:, g * P:g * P + NB + 1],
                                                  rows_f[0:NB + 1, g * P:(g + 1) * P], ident[0:NB + 1, 0:NB + 1])
                    ins.then_inc(s_turned, 1)
                pe.wait_ge(s_cols, 3)
                steps(pe, (3, lambda *b: turn_attr(F, *b)), (2, edge_linear), (0, window_products))
                steps(pe, (AHEAD, lambda *b: project(F, *b)), (0, window_gather), (AHEAD + 1, hidden),
                      (-1, lambda *b: block_sums(e1, F, *b)), (AHEAD + 2, lambda *b: turn_h(F, *b)))
            with pe.Else():
                steps(pe, (1, lambda *b: turn_attr(M, *b)), (1, edge_linear), (0, lambda *b: block_sums(e0, M, *b)))
                steps(pe, (1, lambda *b: turn_h(M, *b)), (1, hidden), (0, lambda *b: project(M, *b)))
                steps(pe, (0, lambda *b: block_sums(e1, M, *b)))


def kernel(x, src, dst, edge_attr_96, edge_weight, L0_gnn_W_edge, L0_gnn_b_edge, L0_gnn_eps, L0_gnn_W1, L0_gnn_b1,
           L0_gnn_W2, L0_gnn_b2):
    import numpy as np
    import concourse.bacc as bacc
    from concourse import mybir as mb
    from concourse.bass_utils import run_bass_kernel_spmd

    laid_out = {
        "x": x, "src": src, "dst": dst, "edge_attr": edge_attr_96, "edge_weight": edge_weight,
        "w_edge_t": np.asarray(L0_gnn_W_edge).T, "b_edge": np.asarray(L0_gnn_b_edge).reshape(1, -1),
        "eps": np.asarray(L0_gnn_eps).reshape(1, 1), "w1_t": np.asarray(L0_gnn_W1).T,
        "b1": np.asarray(L0_gnn_b1).reshape(-1, 1), "w2_t": np.asarray(L0_gnn_W2).T,
        "b2": np.asarray(L0_gnn_b2).reshape(1, -1),
    }
    nc = bacc.Bacc("TRN2", target_bir_lowering=False, num_devices=1)
    arrays, args = {}, []
    for name, a in laid_out.items():
        a = np.ascontiguousarray(a)
        arrays[f"in_{name}"] = a
        args.append(nc.dram_tensor(f"in_{name}", a.shape, mb.dt.from_np(a.dtype), kind="ExternalInput").ap())
    out = nc.dram_tensor("out_h", x.shape, mb.dt.float32, kind="ExternalOutput").ap()
    gnn_kernel(nc, *args, out)
    r = run_bass_kernel_spmd(nc, [arrays], core_ids=[0])
    return r.results[0]["out_h"]
```
